# Optimizing a Trainium2 kernel written in Bass

```python
import numpy as np
import jax
import jax.numpy as jnp

def _softmax(x, axis=-1):
    return jax.nn.softmax(x, axis=axis)

def _gelu(x):
    return jax.nn.gelu(x, approximate=True)

def _silu(x):
    return jax.nn.silu(x)

def _sigmoid(x):
    return jax.nn.sigmoid(x)

def _layernorm(x, axis=-1, eps=1e-05):
    m = jnp.mean(x, axis=axis, keepdims=True)
    v = jnp.var(x, axis=axis, keepdims=True)
    return (x - m) / jnp.sqrt(v + eps)

def _scatter_add(tgt, idx, src, axis=0):
    return tgt.at[idx].add(src)

def _segment_sum(src, seg, n):
    return jax.ops.segment_sum(src, seg, n)
kernel_name = 'mk_flamingo_gated_d1_seqx_r2_27dceb'

def setup_inputs(seed: int=0):
    np.random.seed(seed)
    _w = jnp.asarray

    def _rec_inputs():
        import jax
        import jax.numpy as jnp
        _rk = jax.random.key(seed)
        x = -0.0002928 + 1 * jax.random.normal(jax.random.fold_in(_rk, 1), (64, 256, 512), jnp.float32)
        _lenS = 256 - jax.random.randint(jax.random.fold_in(_rk, 7), (64,), 0, max(1, 256 // 4) + 1, jnp.int32)
        _lenS2 = 256 - jax.random.randint(jax.random.fold_in(_rk, 8), (64,), 0, max(1, 256 // 4) + 1, jnp.int32)
        _ctx_1024P = jax.random.normal(jax.random.fold_in(_rk, 11), (64, 16, 512), jnp.float32)
        _ctx_1024c = jax.random.dirichlet(jax.random.fold_in(_rk, 511), 0.3 * jnp.ones((16,), jnp.float32), (64, 256))
        _ctx_1024t = jnp.einsum('bsk,bkd->bsd', _ctx_1024c, _ctx_1024P)
        _ctx_1024t = _ctx_1024t * jax.lax.rsqrt(jnp.mean(jnp.square(_ctx_1024t)) + 1e-12) * 0.953939
        ctx_1024 = -1.39393e-06 + 0.999914 * (_ctx_1024t + 0.3 * jax.random.normal(jax.random.fold_in(_rk, 611), (64, 256, 512), jnp.float32))
        _g = jax.random.normal(jax.random.fold_in(_rk, 9001), (2, 1), jnp.float32)
        _g = jnp.sign(_g) * jnp.maximum(jnp.abs(_g), 1.0) + (_g == 0) * 1.0
        g_xattn = _g[0]
        g_ffn = _g[1]
        return (x, ctx_1024, g_xattn, g_ffn)
    x, ctx_1024, g_xattn, g_ffn = _rec_inputs()

    def _L0_xattn_setup():
        import jax, jax.numpy as jnp
        import numpy as np
        HIDDEN = 512
        HEADS = 16
        HEAD_DIM = HIDDEN // HEADS
        key = jax.random.key(seed)
        ks = jax.random.split(key, 11)
        B, S = (2, 1024)
        s = 1.0 / np.sqrt(HIDDEN)
        return {'query': jax.random.normal(ks[0], (B, S, HIDDEN), jnp.float32), 'key': jax.random.normal(ks[1], (B, S, HIDDEN), jnp.float32), 'value': jax.random.normal(ks[2], (B, S, HIDDEN), jnp.float32), 'Wq': jax.random.normal(ks[3], (HIDDEN, HIDDEN), jnp.float32) * s, 'bq': jnp.zeros((HIDDEN,), jnp.float32), 'Wk': jax.random.normal(ks[4], (HIDDEN, HIDDEN), jnp.float32) * s, 'bk': jnp.zeros((HIDDEN,), jnp.float32), 'Wv': jax.random.normal(ks[5], (HIDDEN, HIDDEN), jnp.float32) * s, 'bv': jnp.zeros((HIDDEN,), jnp.float32), 'Wo': jax.random.normal(ks[6], (HIDDEN, HIDDEN), jnp.float32) * s, 'bo': jnp.zeros((HIDDEN,), jnp.float32)}
    _L0_xattn_all = _L0_xattn_setup()
    _L0_xattn_in = {k: v for k, v in _L0_xattn_all.items() if k in ('Wq', 'bq', 'Wk', 'bk', 'Wv', 'bv', 'Wo', 'bo')}
    del _L0_xattn_all

    def _L0_ffn_setup():
        import jax, jax.numpy as jnp
        import numpy as np
        DIM = 512

        def _reference_tuple_inner(x, W_r, W_k, W_v, mu_r, mu_k):
            B, T, C = x.shape
            x_prev = jnp.concatenate([jnp.zeros((B, 1, C), x.dtype), x[:, :-1, :]], axis=1)
            xr = mu_r * x + (1.0 - mu_r) * x_prev
            xk = mu_k * x + (1.0 - mu_k) * x_prev
            r = jax.nn.sigmoid(jnp.einsum('btc,dc->btd', xr, W_r))
            k = jnp.einsum('btc,dc->btd', xk, W_k)
            k_act = jnp.square(jax.nn.relu(k))
            out = r * jnp.einsum('btc,dc->btd', k_act, W_v)
            new_state = x[:, -1, :]
            return (out, new_state)
        key = jax.random.key(seed)
        ks = jax.random.split(key, 6)
        B, T, C = (8, 1024, DIM)
        x = jax.random.normal(ks[0], (B, T, C), dtype=jnp.float32)
        s = 1.0 / np.sqrt(C)
        W_r = jax.random.uniform(ks[1], (C, C), jnp.float32, -s, s)
        W_k = jax.random.uniform(ks[2], (C, C), jnp.float32, -s, s)
        W_v = jax.random.uniform(ks[3], (C, C), jnp.float32, -s, s)
        mu_r = jax.random.uniform(ks[4], (C,), jnp.float32)
        mu_k = jax.random.uniform(ks[5], (C,), jnp.float32)
        return {'x': x, 'W_r': W_r, 'W_k': W_k, 'W_v': W_v, 'mu_r': mu_r, 'mu_k': mu_k}
    _L0_ffn_all = _L0_ffn_setup()
    _L0_ffn_in = {k: v for k, v in _L0_ffn_all.items() if k in ('W_r', 'W_k', 'W_v', 'mu_r', 'mu_k')}
    del _L0_ffn_all
    return {'x': x, 'ctx_1024': ctx_1024, 'g_xattn': g_xattn, 'g_ffn': g_ffn, 'L0_xattn_Wq': _L0_xattn_in['Wq'], 'L0_xattn_bq': _L0_xattn_in['bq'], 'L0_xattn_Wk': _L0_xattn_in['Wk'], 'L0_xattn_bk': _L0_xattn_in['bk'], 'L0_xattn_Wv': _L0_xattn_in['Wv'], 'L0_xattn_bv': _L0_xattn_in['bv'], 'L0_xattn_Wo': _L0_xattn_in['Wo'], 'L0_xattn_bo': _L0_xattn_in['bo'], 'L0_ffn_W_r': _L0_ffn_in['W_r'], 'L0_ffn_W_k': _L0_ffn_in['W_k'], 'L0_ffn_W_v': _L0_ffn_in['W_v'], 'L0_ffn_mu_r': _L0_ffn_in['mu_r'], 'L0_ffn_mu_k': _L0_ffn_in['mu_k']}

def reference(x, ctx_1024, g_xattn, g_ffn, L0_xattn_Wq, L0_xattn_bq, L0_xattn_Wk, L0_xattn_bk, L0_xattn_Wv, L0_xattn_bv, L0_xattn_Wo, L0_xattn_bo, L0_ffn_W_r, L0_ffn_W_k, L0_ffn_W_v, L0_ffn_mu_r, L0_ffn_mu_k):
    import jax
    import jax.numpy as jnp

    def _L0_xattn_ref(query, key, value, Wq, bq, Wk, bk, Wv, bv, Wo, bo):
        import jax, jax.numpy as jnp
        import numpy as np
        HIDDEN = 512
        HEADS = 16
        HEAD_DIM = HIDDEN // HEADS
        B, S, _ = query.shape
        Q = query @ Wq.T + bq
        K = key @ Wk.T + bk
        V = value @ Wv.T + bv
        Q = Q.reshape(B, S, HEADS, HEAD_DIM).transpose(0, 2, 1, 3)
        K = K.reshape(B, S, HEADS, HEAD_DIM).transpose(0, 2, 1, 3)
        V = V.reshape(B, S, HEADS, HEAD_DIM).transpose(0, 2, 1, 3)
        scale = jnp.sqrt(jnp.float32(HEAD_DIM))
        energy = jnp.einsum('bhqd,bhkd->bhqk', Q, K) / scale
        attn = jax.nn.softmax(energy, axis=-1)
        x = jnp.einsum('bhqk,bhkd->bhqd', attn, V)
        x = x.transpose(0, 2, 1, 3).reshape(B, S, HIDDEN)
        return x @ Wo.T + bo

    def _L0_ffn_ref(x, W_r, W_k, W_v, mu_r, mu_k):
        import jax, jax.numpy as jnp
        import numpy as np
        DIM = 512

        def _reference_tuple_inner(x, W_r, W_k, W_v, mu_r, mu_k):
            B, T, C = x.shape
            x_prev = jnp.concatenate([jnp.zeros((B, 1, C), x.dtype), x[:, :-1, :]], axis=1)
            xr = mu_r * x + (1.0 - mu_r) * x_prev
            xk = mu_k * x + (1.0 - mu_k) * x_prev
            r = jax.nn.sigmoid(jnp.einsum('btc,dc->btd', xr, W_r))
            k = jnp.einsum('btc,dc->btd', xk, W_k)
            k_act = jnp.square(jax.nn.relu(k))
            out = r * jnp.einsum('btc,dc->btd', k_act, W_v)
            new_state = x[:, -1, :]
            return (out, new_state)
        return _reference_tuple_inner(x, W_r, W_k, W_v, mu_r, mu_k)[0]
    x = x + jnp.tanh(g_xattn[0]) * _L0_xattn_ref(_layernorm(x, axis=-1), ctx_1024, ctx_1024, L0_xattn_Wq, L0_xattn_bq, L0_xattn_Wk, L0_xattn_bk, L0_xattn_Wv, L0_xattn_bv, L0_xattn_Wo, L0_xattn_bo)
    x = x + jnp.tanh(g_ffn[0]) * _L0_ffn_ref(_layernorm(x, axis=-1), L0_ffn_W_r, L0_ffn_W_k, L0_ffn_W_v, L0_ffn_mu_r, L0_ffn_mu_k)
    return x

_drawn_inputs = setup_inputs


def setup_inputs(seed=0):
    import zlib

    import numpy as np

    out = dict(_drawn_inputs(seed))
    spreads = {'L0_xattn_bq': (0.0, 0.52),
     'L0_xattn_bk': (0.0, 0.8),
     'L0_xattn_bv': (0.0, 0.1),
     'L0_xattn_bo': (0.0, 0.1)}
    factors = {'L0_ffn_W_r': 3.339, 'L0_ffn_mu_r': 7.577}
    for name, (base, spread) in spreads.items():
        noise = np.random.default_rng([zlib.crc32(name.encode()), seed]).standard_normal(out[name].shape)
        drawn = base * np.exp(spread * noise) if base else spread * noise
        out[name] = jnp.asarray(drawn.astype(out[name].dtype))
    for name, factor in factors.items():
        out[name] = (out[name] * factor).astype(out[name].dtype)
    return out
```

```python
from contextlib import ExitStack

import concourse.bass as bass
from concourse import mybir


P = 128
BANK = 512
EPS = 1e-5
DMA_INC = 16

ALU = mybir.AluOpType
ACT = mybir.ActivationFunctionType
AX = mybir.AxisListType
F32 = mybir.dt.float32
F32R = mybir.dt.float32r


def attention_pass(nc, psum, x, ctx_t, g, wq_t, bq, wk_t, bk, wv_t, bv, wo_t, bo, eye, x1):
    B, S, D = x.shape
    C = D // P
    HD = 32
    H = D // HD
    HC = P // HD
    T = S // P
    SCALE = float(HD) ** -0.5
    VW = HD + 1
    KROWS = 3 * HD
    MROW = KROWS
    PAIRS = C // 2
    STACK = DMA_INC * HC * 3
    G = H // HC
    assert S == 2 * P and T == 2 and D == BANK and C == 4

    with ExitStack() as weights_scope:
        def wsb(name, shape, dt):
            return weights_scope.enter_context(nc.sbuf_tensor(name, shape, dt))

        w_hi = {n: wsb(f"w{n}_hi", [P, C, D], F32R) for n in "qkvo"}
        w_lo = {n: wsb(f"w{n}_lo", [P, C, D], F32R) for n in "qkvo"}
        eye_sb = wsb("eye_sb", [P, P], F32)
        bq_sb = wsb("bq_sb", [P, C], F32)
        bk_sb = wsb("bk_sb", [P, C], F32)
        out_bias = wsb("out_bias", [P, D], F32)
        minus_half = wsb("minus_half", [P, T], F32)

        with ExitStack() as scope:
            def sb(name, shape, dt):
                return scope.enter_context(nc.sbuf_tensor(name, shape, dt))

            def sem(name):
                return scope.enter_context(nc.semaphore(name))

            raw = {n: sb(f"w{n}_raw", [P, C, D], F32) for n in "qkvo"}
            gate = sb("gate_a", [P, 1], F32)
            bv_sb = sb("bv_sb", [P, C], F32)
            bo_sb = sb("bo_sb", [1, D], F32)
            bias_row = sb("bias_row", [1, D], F32)
            ones_row = sb("ones_row", [1, P], F32)
            w_in = {n: sem(f"w{n}_in") for n in "qkvo"}
            small_in = sem("small_in_a")
            gate_ready = sem("gate_ready_a")
            gated = sem("gated_a")
            hi_ready = sem("w_hi_ready_a")
            lo_ready = sem("w_lo_ready_a")
            ones_ready = sem("ones_ready_a")
            bias_psum = sem("bias_psum")
            bias_ready = sem("bias_ready")
            source = dict(q=wq_t, k=wk_t, v=wv_t, o=wo_t)

            with nc.Block() as block:
                @block.sync
                def _(sp):
                    smalls = [(gate[:, :], g), (bq_sb[:, :], bq), (bk_sb[:, :], bk), (bv_sb[:, :], bv),
                              (bo_sb[:, :], bo), (eye_sb[:, :], eye)]
                    for dst, src in smalls:
                        sp.dma_start(dst, src).then_inc(small_in, DMA_INC)
                    for n in "oqkv":
                        sp.dma_start(raw[n][:, :, :], source[n].rearrange("(c p) n -> p c n", p=P)).then_inc(w_in[n], DMA_INC)

                @block.scalar
                def _(act):
                    act.wait_ge(small_in, 6 * DMA_INC)
                    nc.scalar.activation(gate[:, :], gate[:, :], ACT.Tanh).then_inc(gate_ready, 1)
                    for i, n in enumerate("qkvo"):
                        if n == "o":
                            act.wait_ge(gated, 1)
                        else:
                            act.wait_ge(w_in[n], DMA_INC)
                        nc.scalar.activation(w_hi[n][:, :, :], raw[n][:, :, :], ACT.Copy).then_inc(hi_ready, 1)

                @block.vector
                def _(dve):
                    nc.vector.memset(ones_row[:, :], 1.0).then_inc(ones_ready, 1)
                    nc.vector.memset(minus_half[:, :], -0.5).then_inc(ones_ready, 1)
                    dve.wait_ge(gate_ready, 1)
                    dve.wait_ge(w_in["o"], DMA_INC)
                    nc.vector.tensor_scalar(raw["o"][:, :, :], raw["o"][:, :, :], gate[:, 0:1], None,
                                            ALU.mult).then_inc(gated, 1)
                    for i, n in enumerate("qkvo"):
                        dve.wait_ge(hi_ready, i + 1)
                        nc.vector.tensor_tensor(w_lo[n][:, :, :], raw[n][:, :, :], w_hi[n][:, :, :].bitcast(F32),
                                                ALU.subtract).then_inc(lo_ready, 1)
                    dve.wait_ge(bias_psum, 1)
                    nc.vector.scalar_tensor_tensor(out=bias_row[:, :], in0=bo_sb[:, :], scalar=gate[0:1, 0:1],
                                                   in1=psum[0][0:1, :], op0=ALU.mult, op1=ALU.add).then_inc(bias_ready, 1)
                    dve.wait_ge(bias_psum, 2)
                    nc.vector.tensor_copy(out_bias[:, :], psum[1][:, :]).then_inc(bias_ready, 1)
                    dve.wait_ge(lo_ready, 4)

                @block.tensor
                def _(pe):
                    pe.wait_ge(gated, 1)
                    for c in range(C):
                        last = nc.tensor.matmul(psum[0][0:1, :], bv_sb[:, c:c + 1], raw["o"][:, c, :],
                                                start=(c == 0), stop=(c == C - 1))
                    last.then_inc(bias_psum, 1)
                    pe.wait_ge(ones_ready, 2)
                    pe.wait_ge(bias_ready, 1)
                    nc.tensor.matmul(psum[1][:, :], ones_row[:, :], bias_row[:, :],
                                     start=True, stop=True).then_inc(bias_psum, 1)

        with ExitStack() as scope:
            def sb(name, shape, dt):
                return scope.enter_context(nc.sbuf_tensor(name, shape, dt))

            def sem(name):
                return scope.enter_context(nc.semaphore(name))

            x_sb = [sb(f"x_sb{j}", [P, D], F32) for j in range(T)]
            stats = sb("stats_a", [P, T, 6], F32)
            mean_var = sb("mean_var_a", [P, T, 2], F32)
            var_eps = sb("var_eps_a", [P, T], F32)
            rstd = sb("rstd_a", [P, T], F32)
            xn_hi = sb("xn_hi", [P, C, S], F32R)
            xn_lo = sb("xn_lo", [P, C, S], F32R)
            ctx_raw = sb("ctx_raw", [P, C, S], F32)
            ctx_hi = [sb(f"ctx_hi{i}", [P, C, S], F32R) for i in range(2)]
            ctx_lo = [sb(f"ctx_lo{i}", [P, C, S], F32R) for i in range(2)]
            q_hi = sb("q_hi", [P, C, S], F32R)
            q_lo = sb("q_lo", [P, C, S], F32R)
            k_hi = sb("k_hi", [P, C, S], F32R)
            k_lo = sb("k_lo", [P, C, S], F32R)
            q_stack = [sb(f"q_stack{i}", [P, H, S], F32R) for i in range(2)]
            k_stack = [sb(f"k_stack{i}", [P, H, S], F32R) for i in range(2)]
            v_sb = [sb(f"v_sb{i}", [P, T, H, VW], F32) for i in range(2)]
            row_max = sb("row_max", [P, H, T], F32)
            max_row = sb("max_row", [H * T, P], F32R)
            probs = [sb(f"probs{i}", [P, T, S], F32) for i in range(2)]
            inv_sum = sb("inv_sum", [P, HC, T], F32)
            o_tok = sb("o_tok", [P, T, D], F32)
            o_hi = [sb(f"o_hi{j}", [P, C, P], F32R) for j in range(T)]
            o_lo = [sb(f"o_lo{j}", [P, C, P], F32R) for j in range(T)]
            res = [sb(f"res{j}", [P, D], F32) for j in range(T)]

            acc = psum[0:2]
            s_bank = psum[2:4]
            st_bank = psum[4:6]
            pv_bank = psum[6:8]

            consts = sem("consts")
            x_in = [sem(f"x_in{j}") for j in range(T)]
            ln_step = sem("ln_step")
            rstd_ready = sem("rstd_ready")
            xn_ready = sem("xn_ready")
            xt_psum = sem("xt_psum")
            xt_hi = sem("xt_hi")
            xt_lo = sem("xt_lo")
            ctx_in = sem("ctx_in")
            ctx_hi_ready = sem("ctx_hi_ready")
            ctx_lo_ready = sem("ctx_lo_ready")
            k_psum = sem("k_psum")
            k_hi_ready = sem("k_hi_ready")
            k_lo_ready = sem("k_lo_ready")
            q_psum = sem("q_psum")
            q_hi_ready = sem("q_hi_ready")
            q_lo_ready = sem("q_lo_ready")
            k_stacked = [sem(f"k_stacked{i}") for i in range(PAIRS)]
            q_stacked = [sem(f"q_stacked{i}") for i in range(PAIRS)]
            v_psum = sem("v_psum")
            v_ready = sem("v_ready")
            s_psum = sem("s_psum")
            max_ready = sem("max_ready")
            max_psum = sem("max_psum")
            max_copied = sem("max_copied")
            max_stacked = sem("max_stacked")
            st_psum = sem("st_psum")
            probs_ready = sem("probs_ready")
            pv_psum = sem("pv_psum")
            inv_ready = sem("inv_ready")
            o_ready = sem("o_ready")
            ot_psum = sem("ot_psum")
            ot_hi = sem("ot_hi")
            ot_lo = sem("ot_lo")
            o_psum = sem("o_psum")
            res_in = [sem(f"res_in{j}") for j in range(T)]
            res_biased = sem("res_biased")
            x1_ready = sem("x1_ready")
            x1_out = [sem(f"x1_out{j}") for j in range(T)]

            FIRST_STEADY = 4
            LAST_STEADY = B - 2
            assert (LAST_STEADY - FIRST_STEADY) % 2 == 0

            def run(eng, step):
                for s in range(-1, FIRST_STEADY):
                    step(s, s)
                with eng.Fori(0, (LAST_STEADY - FIRST_STEADY) // 2) as i:
                    for j in range(2):
                        step(2 * i + (FIRST_STEADY + j), FIRST_STEADY + j)
                for s in range(LAST_STEADY, B + 4):
                    step(s, s)

            def has(n):
                return 0 <= n < B

            block = scope.enter_context(nc.Block())

            @block.sync
            def _(sp):
                def stack(b, n, pair, hi, lo, dst, order, ready, stacked):
                    if n >= 2 and dst is k_stack:
                        sp.wait_ge(st_psum, H * (b - 2) + (pair + 1) * H // PAIRS)
                    sp.wait_ge(ready, 2 * b + pair + 1)
                    rows = dst[n % 2][:, :, :].rearrange("p (c j) t -> p c j t", j=HC)
                    cs = slice(2 * pair, 2 * pair + 2)
                    for j in range(HC):
                        for i, part in enumerate(order):
                            src = (hi, lo)[part]
                            sp.dma_start(rows[HD * i:HD * i + HD, cs, j, :].bitcast(F32),
                                         src[HD * j:HD * j + HD, cs, :].bitcast(F32)).then_inc(stacked[pair], DMA_INC)

                def stack_k(b, n, pair):
                    stack(b, n, pair, k_hi, k_lo, k_stack, (0, 1, 0), k_lo_ready, k_stacked)

                def stack_q(b, n, pair):
                    stack(b, n, pair, q_hi, q_lo, q_stack, (0, 0, 1), q_lo_ready, q_stacked)

                def store(b, j):
                    sp.wait_ge(x1_ready, 2 * b + j + 1)
                    sp.dma_start(x1[b, j * P:(j + 1) * P, :], res[j][:, :]).then_inc(x1_out[j], DMA_INC)

                def step(s, n):
                    if has(n - 1):
                        stack_k(s - 1, n - 1, 1)
                        stack_q(s - 1, n - 1, 1)
                    if has(n - 4):
                        store(s - 4, 1)
                    if has(n + 1):
                        for j in range(T):
                            if n >= 0:
                                sp.wait_ge(xt_psum, 2 * s + j + 1)
                            sp.dma_start(x_sb[j][:, :], x[s + 1, j * P:(j + 1) * P, :]).then_inc(x_in[j], DMA_INC)
                        if n >= 0:
                            sp.wait_ge(ctx_lo_ready, s + 1)
                        sp.dma_start(ctx_raw[:, :, :], ctx_t[s + 1, :, :].rearrange("(c p) t -> p c t", p=P))\
                            .then_inc(ctx_in, DMA_INC)
                    if has(n - 3):
                        for j in range(T):
                            if n >= 4:
                                sp.wait_ge(x1_out[j], DMA_INC * (s - 3))
                            sp.dma_start(res[j][:, :], x[s - 3, j * P:(j + 1) * P, :]).then_inc(res_in[j], DMA_INC)
                    if has(n):
                        stack_k(s, n, 0)
                        stack_q(s, n, 0)
                    if has(n - 3):
                        store(s - 3, 0)

                run(sp, step)
                for j in range(T):
                    sp.wait_ge(x1_out[j], DMA_INC * B)

            @block.gpsimd
            def _(pool):
                def step(s, n):
                    if has(n - 3):
                        for j in range(T):
                            pool.wait_ge(res_in[j], DMA_INC * (s - 2))
                            nc.gpsimd.tensor_tensor(res[j][:, :], res[j][:, :], out_bias[:, :], ALU.add)\
                                .then_inc(res_biased, 1)
                    if has(n + 1):
                        pool.wait_ge(ctx_hi_ready, s + 2)
                        i = (n + 1) % 2
                        nc.gpsimd.tensor_tensor(ctx_lo[i][:, :, :], ctx_raw[:, :, :], ctx_hi[i][:, :, :].bitcast(F32),
                                                ALU.subtract).then_inc(ctx_lo_ready, 1)
                        pool.wait_ge(ln_step, 5 * (s + 2))
                        nc.gpsimd.tensor_tensor(rstd[:, :], var_eps[:, :], minus_half[:, :], ALU.pow)\
                            .then_inc(rstd_ready, 1)

                run(pool, step)

            @block.scalar
            def _(act):
                def exp(b, n, u):
                    act.wait_ge(st_psum, H * b + u + 1)
                    if n > 0 or u >= 2:
                        act.wait_ge(pv_psum, H * b + u - 1)
                    nc.scalar.activation(probs[u % 2][:, :, :].rearrange("p a t -> p (a t)"), st_bank[u % 2][:, :],
                                         ACT.Exp, scale=SCALE).then_inc(probs_ready, 1)

                def transposed_hi(b, n, j):
                    act.wait_ge(xt_psum, 2 * b + j + 1)
                    if n > 0:
                        act.wait_ge(q_psum, 2 * b)
                    nc.scalar.activation(xn_hi[:, :, j * P:(j + 1) * P], acc[1 - j][:, :].rearrange("p (c t) -> p c t", c=C),
                                         ACT.Copy).then_inc(xt_hi, 1)

                def projected_hi(b, n, pair, out, bias, bank, done, stacked, ready):
                    act.wait_ge(done, 2 * b + pair + 1)
                    if n > 0:
                        act.wait_ge(stacked[pair], STACK * b)
                    for c in range(2 * pair, 2 * pair + 2):
                        at = (c % 2) * S
                        last = nc.scalar.activation(out[:, c, :], bank[:, at:at + S], ACT.Identity, bias=bias[:, c:c + 1])
                    last.then_inc(ready, 1)

                def values(b, n, j):
                    act.wait_ge(v_psum, 2 * b + j + 1)
                    if n >= 2:
                        act.wait_ge(pv_psum, H * (b - 1))
                    nc.scalar.activation(v_sb[n % 2][:, j, :, 0:HD], acc[j][:, :].rearrange("p (h d) -> p h d", h=H),
                                         ACT.Copy).then_inc(v_ready, 1)

                def output_hi(b, n, j):
                    act.wait_ge(ot_psum, 2 * b + j + 1)
                    if n > 0:
                        act.wait_ge(o_psum, 2 * b + j - 1)
                    nc.scalar.activation(o_hi[j][:, :, :], acc[1 - j][:, :].rearrange("p (c t) -> p c t", c=C),
                                         ACT.Copy).then_inc(ot_hi, 1)

                def step(s, n):
                    for k in range(H):
                        if has(n - 2):
                            exp(s - 2, n - 2, k)
                        if k in (1, 3) and has(n):
                            transposed_hi(s, n, k // 2)
                        if k in (2, 4) and has(n):
                            projected_hi(s, n, k // 2 - 1, k_hi, bk_sb, acc[k // 2 - 1], k_psum, k_stacked, k_hi_ready)
                        if k in (5, 7) and has(n - 3):
                            output_hi(s - 3, n - 3, (k - 5) // 2)
                        if k in (6, 8) and has(n - 1):
                            values(s - 1, n - 1, (k - 6) // 2)
                        if k == 9 and has(n + 1):
                            act.wait_ge(ctx_in, DMA_INC * (s + 2))
                            if n >= 1:
                                act.wait_ge(v_psum, 2 * s)
                            nc.scalar.activation(ctx_hi[(n + 1) % 2][:, :, :], ctx_raw[:, :, :], ACT.Copy)\
                                .then_inc(ctx_hi_ready, 1)
                        if k in (10, 12) and has(n):
                            i = (k - 10) // 2
                            projected_hi(s, n, i, q_hi, bq_sb, acc[i], q_psum, q_stacked, q_hi_ready)
                        if k == 13 and has(n - 1):
                            act.wait_ge(max_copied, s)
                            act.dma_start(q_stack[(n - 1) % 2][MROW:MROW + 1, :, :].rearrange("o h (j t) -> o (h j) t", j=T).bitcast(F32),
                                          max_row[:, :].bitcast(F32)).then_inc(max_stacked, DMA_INC)

                run(act, step)

            @block.vector
            def _(dve):
                for i in range(2):
                    nc.vector.memset(v_sb[i][:, :, :, HD:VW], 1.0).then_inc(consts, 1)
                    nc.vector.memset(k_stack[i][MROW:MROW + 1, :, :].bitcast(F32), -1.0).then_inc(consts, 1)

                def residual(b, j):
                    dve.wait_ge(o_psum, 2 * b + j + 1)
                    dve.wait_ge(res_biased, 2 * b + j + 1)
                    nc.vector.tensor_tensor(res[j][:, :], acc[j][:, :], res[j][:, :], ALU.add).then_inc(x1_ready, 1)

                def normalise(b, n, grp):
                    bank = pv_bank[grp % 2][:, 0:HC * T * VW].rearrange("p (h j v) -> p h j v", h=HC, j=T)
                    dve.wait_ge(pv_psum, H * b + HC * (grp + 1))
                    if n > 0 or grp > 0:
                        dve.wait_ge(o_ready, G * b + grp)
                    nc.vector.reciprocal(inv_sum[:, :, :], bank[:, :, :, HD]).then_inc(inv_ready, 1)
                    if n > 0 and grp == 0:
                        dve.wait_ge(ot_psum, 2 * b)
                    dve.wait_ge(inv_ready, G * b + grp + 1)
                    out = o_tok[:, :, grp * P:(grp + 1) * P].rearrange("p j (h d) -> p h j d", h=HC)
                    nc.vector.tensor_tensor(out, bank[:, :, :, 0:HD],
                                            inv_sum[:, :, :].unsqueeze(3).to_broadcast([P, HC, T, HD]),
                                            ALU.mult).then_inc(o_ready, 1)

                def transposed_lo(b, j):
                    dve.wait_ge(xt_hi, 2 * b + j + 1)
                    at = slice(j * P, (j + 1) * P)
                    nc.vector.tensor_tensor(xn_lo[:, :, at], acc[1 - j][:, :].rearrange("p (c t) -> p c t", c=C),
                                            xn_hi[:, :, at].bitcast(F32), ALU.subtract).then_inc(xt_lo, 1)

                def projected_lo(b, pair, hi, lo, bias, bank, hi_ready, lo_ready):
                    dve.wait_ge(hi_ready, 2 * b + pair + 1)
                    for c in range(2 * pair, 2 * pair + 2):
                        at = (c % 2) * S
                        last = nc.vector.scalar_tensor_tensor(out=lo[:, c, :], in0=bank[:, at:at + S],
                                                              scalar=bias[:, c:c + 1], in1=hi[:, c, :].bitcast(F32),
                                                              op0=ALU.add, op1=ALU.subtract)
                    last.then_inc(lo_ready, 1)

                def output_lo(b, j):
                    dve.wait_ge(ot_hi, 2 * b + j + 1)
                    nc.vector.tensor_tensor(o_lo[j][:, :, :], acc[1 - j][:, :].rearrange("p (c t) -> p c t", c=C),
                                            o_hi[j][:, :, :].bitcast(F32), ALU.subtract).then_inc(ot_lo, 1)

                def maximum(b, n, u):
                    dve.wait_ge(s_psum, H * b + u + 1)
                    if n > 0 and u == 0:
                        dve.wait_ge(max_psum, b)
                    nc.vector.tensor_reduce(row_max[:, u, :], s_bank[u % 2][:, :].rearrange("p (j t) -> p j t", j=T),
                                            AX.X, ALU.max).then_inc(max_ready, 1)

                def statistics(b, n):
                    if n > 0:
                        dve.wait_ge(ln_step, 5 * b)
                    for j in range(T):
                        dve.wait_ge(x_in[j], DMA_INC * (b + 1))
                        nc.vector.bn_stats(stats[:, j, :], x_sb[j][:, :]).then_inc(ln_step, 1)

                def variance(b):
                    for j in range(T):
                        nc.vector.bn_aggr(mean_var[:, j, :], stats[:, j, :]).then_inc(ln_step, 1)
                    dve.wait_ge(ln_step, 5 * b + 2 * T)
                    nc.vector.tensor_scalar(var_eps[:, :], mean_var[:, :, 1], EPS, None, ALU.add).then_inc(ln_step, 1)

                def layer_norm(b):
                    dve.wait_ge(rstd_ready, b + 1)
                    for j in range(T):
                        nc.vector.tensor_scalar(x_sb[j][:, :], x_sb[j][:, :], mean_var[:, j, 0:1], rstd[:, j:j + 1],
                                                ALU.subtract, ALU.mult).then_inc(xn_ready, 1)

                def step(s, n):
                    for k in range(H):
                        if k == 0 and has(n - 4):
                            residual(s - 4, 1)
                        if k == 1 and has(n - 3):
                            normalise(s - 3, n - 3, G - 1)
                        if k in (8, 10, 13) and has(n - 2):
                            normalise(s - 2, n - 2, (8, 10, 13).index(k))
                        if k in (1, 3) and has(n):
                            transposed_lo(s, k // 2)
                        if k in (2, 4) and has(n):
                            i = k // 2 - 1
                            projected_lo(s, i, k_hi, k_lo, bk_sb, acc[i], k_hi_ready, k_lo_ready)
                        if 3 <= k < 11 and has(n - 1):
                            maximum(s - 1, n - 1, 2 * (k - 3))
                            maximum(s - 1, n - 1, 2 * (k - 3) + 1)
                        if k in (5, 7) and has(n - 3):
                            output_lo(s - 3, (k - 5) // 2)
                        if k in (10, 12) and has(n):
                            i = (k - 10) // 2
                            projected_lo(s, i, q_hi, q_lo, bq_sb, acc[i], q_hi_ready, q_lo_ready)
                        if k == 11 and has(n + 1):
                            statistics(s + 1, n + 1)
                        if k == 12 and has(n + 1):
                            dve.wait_ge(ln_step, 5 * (s + 1) + T)
                            if n >= 0:
                                dve.wait_ge(xn_ready, 2 * (s + 1))
                        if k == 12 and has(n - 1):
                            dve.wait_ge(max_psum, s)
                            if n >= 2:
                                dve.wait_ge(max_stacked, DMA_INC * (s - 1))
                            nc.vector.tensor_copy(max_row[:, :], s_bank[0][0:H * T, 0:P]).then_inc(max_copied, 1)
                        if k == 12 and has(n + 1):
                            variance(s + 1)
                        if k == 13 and has(n + 1):
                            layer_norm(s + 1)
                        if k == 14 and has(n - 3):
                            residual(s - 3, 0)

                run(dve, step)

            @block.tensor
            def _(pe):
                def scores_t(b, n, u):
                    if u == 0:
                        pe.wait_ge(max_stacked, DMA_INC * (b + 1))
                    if n > 0 or u >= 2:
                        pe.wait_ge(probs_ready, H * b + u - 1)
                    for t in range(T):
                        last = nc.tensor.matmul(st_bank[u % 2][:, t * S:(t + 1) * S],
                                                k_stack[n % 2][0:MROW + 1, u, t * P:(t + 1) * P],
                                                q_stack[n % 2][0:MROW + 1, u, :], start=True, stop=True)
                    last.then_inc(st_psum, 1)

                def weighted(b, n, u):
                    grp = u // HC
                    if u == 0:
                        pe.wait_ge(v_ready, 2 * b + 2)
                    if u % HC == 0 and (n > 0 or grp >= 2):
                        pe.wait_ge(o_ready, G * b + grp - 1)
                    pe.wait_ge(probs_ready, H * b + u + 1)
                    for j in range(T):
                        at = ((u % HC) * T + j) * VW
                        for t in range(T):
                            last = nc.tensor.matmul(pv_bank[grp % 2][:, at:at + VW],
                                                    probs[u % 2][:, t, j * P:(j + 1) * P],
                                                    v_sb[n % 2][:, t, u, :], start=(t == 0), stop=(t == T - 1))
                    last.then_inc(pv_psum, 1)

                def scores(b, n, u):
                    if u == 0:
                        pe.wait_ge(k_stacked[0], STACK * (b + 1))
                        pe.wait_ge(q_stacked[0], STACK * (b + 1))
                        if n > 0:
                            pe.wait_ge(max_copied, b)
                    elif u == H // 2:
                        pe.wait_ge(k_stacked[1], STACK * (b + 1))
                        pe.wait_ge(q_stacked[1], STACK * (b + 1))
                    if n > 0 or u >= 2:
                        pe.wait_ge(max_ready, H * b + u - 1)
                    for j in range(T):
                        last = nc.tensor.matmul(s_bank[u % 2][:, j * S:(j + 1) * S],
                                                q_stack[n % 2][0:KROWS, u, j * P:(j + 1) * P],
                                                k_stack[n % 2][0:KROWS, u, :], start=True, stop=True)
                    last.then_inc(s_psum, 1)

                def maxima(b, n):
                    pe.wait_ge(max_ready, H * (b + 1))
                    nc.tensor.transpose(s_bank[0][0:H * T, 0:P], row_max[:, :, :].rearrange("p h j -> p (h j)"),
                                        eye_sb[:, :]).then_inc(max_psum, 1)

                def transpose_x(s, n, j):
                    if j == 0:
                        if has(n - 4):
                            pe.wait_ge(x1_ready, 2 * (s - 4) + 2)
                        elif n >= 1:
                            pe.wait_ge(q_lo_ready, 2 * s)
                    else:
                        pe.wait_ge(k_lo_ready, 2 * s + 1)
                    pe.wait_ge(xn_ready, 2 * s + j + 1)
                    for c in range(C):
                        last = nc.tensor.transpose(acc[1 - j][:, c * P:(c + 1) * P], x_sb[j][:, c * P:(c + 1) * P],
                                                   eye_sb[:, :])
                    last.then_inc(xt_psum, 1)

                def transposed_product(w, act_hi, act_lo, pair, bank, half):
                    c = 2 * pair + half
                    cols = slice(c * P, (c + 1) * P)
                    out = bank[:, half * S:(half + 1) * S]
                    for i in range(C):
                        nc.tensor.matmul(out, w_hi[w][:, i, cols], act_hi[:, i, :], start=(i == 0), stop=False)
                        nc.tensor.matmul(out, w_hi[w][:, i, cols], act_lo[:, i, :], start=False, stop=False)
                        last = nc.tensor.matmul(out, w_lo[w][:, i, cols], act_hi[:, i, :], start=False, stop=(i == C - 1))
                    return last

                def keys(s, n, pair, half):
                    if half == 0:
                        if pair == 0:
                            pe.wait_ge(ctx_lo_ready, s + 1)
                            if has(n - 4):
                                pe.wait_ge(x1_ready, 2 * (s - 4) + 1)
                            elif n >= 1:
                                pe.wait_ge(q_lo_ready, 2 * s - 1)
                        else:
                            pe.wait_ge(xt_lo, 2 * s + 1)
                    last = transposed_product("k", ctx_hi[n % 2], ctx_lo[n % 2], pair, acc[pair], half)
                    if half == 1:
                        last.then_inc(k_psum, 1)

                def queries(s, n, pair, half):
                    if half == 0:
                        if pair == 0:
                            pe.wait_ge(xt_lo, 2 * s + 2)
                            if has(n - 3):
                                pe.wait_ge(ot_lo, 2 * (s - 3) + 2)
                            elif has(n - 1):
                                pe.wait_ge(v_ready, 2 * s - 1)
                        elif has(n - 1):
                            pe.wait_ge(v_ready, 2 * s)
                        else:
                            pe.wait_ge(k_lo_ready, 2 * s + 2)
                    last = transposed_product("q", xn_hi, xn_lo, pair, acc[pair], half)
                    if half == 1:
                        last.then_inc(q_psum, 1)

                def token_product(w, act_hi, act_lo, bank, half, start, stop):
                    for i in (2 * half, 2 * half + 1):
                        nc.tensor.matmul(bank[:, :], act_hi(i), w_hi[w][:, i, :], start=(start and i == 0), stop=False)
                        nc.tensor.matmul(bank[:, :], act_hi(i), w_lo[w][:, i, :], start=False, stop=False)
                        last = nc.tensor.matmul(bank[:, :], act_lo(i), w_hi[w][:, i, :], start=False,
                                                stop=(stop and i == C - 1))
                    return last

                def values(s, n, j, half):
                    if half == 0:
                        if j == 0:
                            if has(n):
                                pe.wait_ge(xt_lo, 2 * s + 2)
                            else:
                                pe.wait_ge(x1_ready, 2 * (s - 4) + 1)
                        elif has(n - 3):
                            pe.wait_ge(ot_lo, 2 * (s - 3) + 1)
                        else:
                            pe.wait_ge(k_lo_ready, 2 * s + 2)
                    par, at = (n - 1) % 2, slice(j * P, (j + 1) * P)
                    last = token_product("v", lambda i: ctx_hi[par][:, i, at], lambda i: ctx_lo[par][:, i, at],
                                         acc[j], half, True, True)
                    if half == 1:
                        last.then_inc(v_psum, 1)

                def transpose_o(s, n, j):
                    if j == 0:
                        if has(n):
                            pe.wait_ge(k_lo_ready, 2 * s + 2)
                        elif has(n - 4):
                            pe.wait_ge(x1_ready, 2 * (s - 4) + 2)
                        pe.wait_ge(o_ready, G * (s - 2))
                    elif has(n - 1):
                        pe.wait_ge(v_ready, 2 * s - 1)
                    elif has(n - 4):
                        pe.wait_ge(x1_ready, 2 * (s - 4) + 1)
                    for c in range(C):
                        last = nc.tensor.transpose(acc[1 - j][:, c * P:(c + 1) * P], o_tok[:, j, c * P:(c + 1) * P],
                                                   eye_sb[:, :])
                    last.then_inc(ot_psum, 1)

                def output(s, n, j, half):
                    if half == 0:
                        pe.wait_ge(ot_lo, 2 * (s - 3) + (2 if j == 0 else 2))
                        if has(n):
                            pe.wait_ge(q_lo_ready, 2 * s + j + 1)
                        elif has(n - 1) and j == 1:
                            pe.wait_ge(v_ready, 2 * s)
                    last = token_product("o", lambda i: o_hi[j][:, i, :], lambda i: o_lo[j][:, i, :],
                                         acc[j], half, True, True)
                    if half == 1:
                        last.then_inc(o_psum, 1)

                def step(s, n):
                    for k in range(H):
                        if has(n - 2):
                            scores_t(s - 2, n - 2, k)
                        if k == 0 and has(n - 3):
                            weighted(s - 3, n - 3, H - 1)
                        if k > 0 and has(n - 2):
                            weighted(s - 2, n - 2, k - 1)
                        if k in (1, 3) and has(n):
                            transpose_x(s, n, k // 2)
                        if k in (5, 7) and has(n - 3):
                            transpose_o(s, n, (k - 5) // 2)
                        if 3 <= k < 11 and has(n - 1):
                            scores(s - 1, n - 1, 2 * (k - 3))
                            scores(s - 1, n - 1, 2 * (k - 3) + 1)
                        if k == 12 and has(n - 1):
                            maxima(s - 1, n - 1)
                        if k < 4 and has(n):
                            keys(s, n, k // 2, k % 2)
                        if 4 <= k < 8 and has(n - 1):
                            values(s, n, (k - 4) // 2, k % 2)
                        if 8 <= k < 12 and has(n):
                            queries(s, n, (k - 8) // 2, k % 2)
                        if k >= 12 and has(n - 3):
                            output(s, n, (k - 12) // 2, k % 2)

                pe.wait_ge(consts, 4)
                run(pe, step)


def channel_mix_pass(nc, psum, x1, g, wr_t, wk_t, wv_t, mu_r, mu_k, eye, out):
    B, S, D = x1.shape
    C = D // P
    TP = 2 * S
    T = TP // P
    STEPS = B // 2
    assert TP == BANK and C == 4 and T == 4

    with ExitStack() as weights_scope:
        def wsb(name, shape, dt):
            return weights_scope.enter_context(nc.sbuf_tensor(name, shape, dt))

        w_hi = {n: wsb(f"f{n}_hi", [P, C, D], F32R) for n in "rkv"}
        w_lo = {n: wsb(f"f{n}_lo", [P, C, D], F32R) for n in "rkv"}
        eye_sb = wsb("eye_f", [P, P], F32)
        mu = {n: wsb(f"mu_{n}_sb", [P, C], F32) for n in "rk"}
        one_minus_mu = {n: wsb(f"one_minus_mu_{n}", [P, C], F32) for n in "rk"}
        minus_half = wsb("minus_half_f", [P, T], F32)

        with ExitStack() as scope:
            def sem(name):
                return scope.enter_context(nc.semaphore(name))

            raw = {n: scope.enter_context(nc.sbuf_tensor(f"f{n}_raw", [P, C, D], F32)) for n in "rkv"}
            gate = scope.enter_context(nc.sbuf_tensor("gate_f", [P, 1], F32))
            w_in = {n: sem(f"f{n}_in") for n in "rkv"}
            small_in = sem("small_in_f")
            gate_ready = sem("gate_ready_f")
            gated = sem("gated_f")
            hi_ready = sem("w_hi_ready_f")
            lo_ready = sem("w_lo_ready_f")
            source = dict(r=wr_t, k=wk_t, v=wv_t)

            with nc.Block() as block:
                @block.sync
                def _(sp):
                    for dst, src in ((gate, g), (mu["r"], mu_r), (mu["k"], mu_k), (eye_sb, eye)):
                        sp.dma_start(dst[:, :], src).then_inc(small_in, DMA_INC)
                    for n in "kvr":
                        sp.dma_start(raw[n][:, :, :], source[n].rearrange("(c p) n -> p c n", p=P)).then_inc(w_in[n], DMA_INC)

                @block.scalar
                def _(act):
                    act.wait_ge(small_in, 4 * DMA_INC)
                    nc.scalar.activation(gate[:, :], gate[:, :], ACT.Tanh).then_inc(gate_ready, 1)
                    for n in "krv":
                        if n == "v":
                            act.wait_ge(gated, 1)
                        else:
                            act.wait_ge(w_in[n], DMA_INC)
                        nc.scalar.activation(w_hi[n][:, :, :], raw[n][:, :, :], ACT.Copy).then_inc(hi_ready, 1)

                @block.vector
                def _(dve):
                    nc.vector.memset(minus_half[:, :], -0.5).then_inc(lo_ready, 1)
                    dve.wait_ge(small_in, 4 * DMA_INC)
                    for n in "rk":
                        nc.vector.tensor_scalar(one_minus_mu[n][:, :], mu[n][:, :], -1.0, 1.0, ALU.mult, ALU.add)\
                            .then_inc(lo_ready, 1)
                    dve.wait_ge(gate_ready, 1)
                    dve.wait_ge(w_in["v"], DMA_INC)
                    nc.vector.tensor_scalar(raw["v"][:, :, :], raw["v"][:, :, :], gate[:, 0:1], 0.5,
                                            ALU.mult, ALU.mult).then_inc(gated, 1)
                    for i, n in enumerate("krv"):
                        dve.wait_ge(hi_ready, i + 1)
                        nc.vector.tensor_tensor(w_lo[n][:, :, :], raw[n][:, :, :], w_hi[n][:, :, :].bitcast(F32),
                                                ALU.subtract).then_inc(lo_ready, 1)
                    dve.wait_ge(lo_ready, 6)

        with ExitStack() as scope:
            def sb(name, shape, dt):
                return scope.enter_context(nc.sbuf_tensor(name, shape, dt))

            def sem(name):
                return scope.enter_context(nc.semaphore(name))

            x_sb = [[sb(f"y{i}_sb{j}", [P, D], F32) for j in range(T)] for i in range(2)]
            stats = sb("stats_f", [P, T, 6], F32)
            mean_var = sb("mean_var_f", [P, T, 2], F32)
            var_eps = sb("var_eps_f", [P, T], F32)
            rstd = sb("rstd_f", [P, T], F32)
            xn = sb("xn_f", [P, T, D], F32)
            xt = sb("xt_f", [P, C, 2, S + 1], F32)
            mixed = {n: sb(f"mixed_{n}", [P, C, TP], F32) for n in "rk"}
            m_hi = {n: sb(f"m{n}_hi", [P, C, TP], F32R) for n in "rk"}
            m_lo = {n: sb(f"m{n}_lo", [P, C, TP], F32R) for n in "rk"}
            kact = sb("kact", [P, C, TP], F32)
            kact_hi = sb("kact_hi", [P, C, TP], F32R)
            kact_lo = sb("kact_lo", [P, C, TP], F32R)
            tanh_r = sb("tanh_r", [P, T, D], F32)

            kv_bank = psum[0:4]
            r_bank = psum[4:6]
            t_bank = psum[6:8]

            zeroed = sem("zeroed")
            x_in = [[sem(f"y{i}_in{j}") for j in range(T)] for i in range(2)]
            ln_step = sem("ln_step_f")
            rstd_ready = sem("rstd_ready_f")
            xn_ready = sem("xn_ready_f")
            xt_psum = sem("xt_psum_f")
            xt_ready = sem("xt_ready_f")
            k_mixed = sem("k_mixed")
            k_hi = sem("k_hi_f")
            k_lo = sem("k_lo_f")
            r_mixed = sem("r_mixed")
            r_hi = sem("r_hi_f")
            r_lo = sem("r_lo_f")
            k_psum = sem("k_psum_f")
            relu_ready = sem("relu_ready")
            square_ready = sem("square_ready")
            act_hi = sem("act_hi")
            act_lo = sem("act_lo")
            r_psum = sem("r_psum")
            tanh_ready = sem("tanh_ready")
            v_psum = sem("v_psum_f")
            product_ready = sem("product_ready")
            out_ready = sem("out_ready")
            out_sent = [sem(f"out_sent{j}") for j in range(T)]

            FIRST_STEADY = 2
            LAST_STEADY = STEPS - 2
            assert (LAST_STEADY - FIRST_STEADY) % 2 == 0

            def run(eng, step):
                for s in range(-1, FIRST_STEADY):
                    step(s, s)
                with eng.Fori(0, (LAST_STEADY - FIRST_STEADY) // 2) as i:
                    for j in range(2):
                        step(2 * i + (FIRST_STEADY + j), FIRST_STEADY + j)
                for s in range(LAST_STEADY, STEPS):
                    step(s, s)

            def has(n):
                return 0 <= n < STEPS

            def rows(dram, s, j):
                return dram[2 * s + j // 2, (j % 2) * P:(j % 2 + 1) * P, :]

            block = scope.enter_context(nc.Block())

            @block.sync
            def _(sp):
                for j in range(T):
                    sp.dma_start(x_sb[0][j][:, :], rows(x1, 0, j)).then_inc(x_in[0][j], DMA_INC)

                def step(s, n):
                    for j in range(T):
                        if has(n):
                            sp.wait_ge(out_ready, T * s + j + 1)
                            sp.dma_start(rows(out, s, j), tanh_r[:, j, :]).then_inc(out_sent[j], DMA_INC)
                        if has(n + 2):
                            sp.dma_start(x_sb[n % 2][j][:, :], rows(x1, s + 2, j)).then_inc(x_in[n % 2][j], DMA_INC)

                run(sp, step)
                for j in range(T):
                    sp.wait_ge(out_sent[j], DMA_INC * STEPS)

            @block.gpsimd
            def _(pool):
                def step(s, n):
                    for c in range(C):
                        if has(n):
                            pool.wait_ge(relu_ready, C * s + c + 1)
                            nc.gpsimd.tensor_tensor(kact[:, c, :], kact[:, c, :], kact[:, c, :], ALU.mult)\
                                .then_inc(square_ready, 1)
                        if c == 0 and has(n + 1):
                            pool.wait_ge(ln_step, 9 * (s + 2))
                            nc.gpsimd.tensor_tensor(rstd[:, :], var_eps[:, :], minus_half[:, :], ALU.pow)\
                                .then_inc(rstd_ready, 1)
                    if has(n):
                        for j in range(T):
                            pool.wait_ge(product_ready, T * s + j + 1)
                            nc.gpsimd.tensor_tensor(tanh_r[:, j, :], tanh_r[:, j, :], x_sb[n % 2][j][:, :], ALU.add)\
                                .then_inc(out_ready, 1)

                run(pool, step)

            @block.scalar
            def _(act):
                def relu(s, n, c):
                    act.wait_ge(k_psum, C * s + c + 1)
                    if n > 0:
                        act.wait_ge(act_lo, C * s + c - C + 1)
                    nc.scalar.activation(kact[:, c, :], kv_bank[c][:, :], ACT.Relu).then_inc(relu_ready, 1)

                def square_hi(s, n, c):
                    act.wait_ge(square_ready, C * s + c + 1)
                    if n > 0:
                        act.wait_ge(v_psum, T * s)
                    nc.scalar.activation(kact_hi[:, c, :], kact[:, c, :], ACT.Copy).then_inc(act_hi, 1)

                def tanh(s, n, j):
                    act.wait_ge(r_psum, T * s + j + 1)
                    if n > 0:
                        act.wait_ge(out_sent[j], DMA_INC * s)
                    nc.scalar.activation(tanh_r[:, j, :], r_bank[j % 2][:, :], ACT.Tanh, scale=0.5)\
                        .then_inc(tanh_ready, 1)

                def transposed(s, n, c):
                    bank = t_bank[c % 2][:, :]
                    act.wait_ge(xt_psum, C * s + c + 1)
                    if n > 0:
                        act.wait_ge(r_lo, C * s - C + c + 1)
                    nc.scalar.activation(xt[:, c, :, 1:S + 1], bank.rearrange("p (b t) -> p b t", b=2), ACT.Copy)
                    nc.scalar.activation(mixed["k"][:, c, :], bank, ACT.Copy, scale=mu["k"][:, c:c + 1])
                    nc.scalar.activation(mixed["r"][:, c, :], bank, ACT.Copy, scale=mu["r"][:, c:c + 1])\
                        .then_inc(xt_ready, 1)

                def mixed_hi(s, n, c):
                    act.wait_ge(r_mixed, C * s + c + 1)
                    nc.scalar.activation(m_hi["r"][:, c, :], mixed["r"][:, c, :], ACT.Copy).then_inc(r_hi, 1)

                def step(s, n):
                    if has(n):
                        for c in range(C):
                            relu(s, n, c)
                            if c >= 1:
                                square_hi(s, n, c - 1)
                    for c in range(C):
                        if has(n):
                            tanh(s, n, c)
                            if c == 0:
                                square_hi(s, n, C - 1)
                        if has(n + 1):
                            transposed(s + 1, n + 1, c)
                    if has(n + 1):
                        for c in range(C):
                            mixed_hi(s + 1, n + 1, c)

                run(act, step)

            @block.vector
            def _(dve):
                nc.vector.memset(xt[:, :, :, 0:1], 0.0).then_inc(zeroed, 1)

                def statistics(s, n):
                    x = x_sb[n % 2]
                    if n > 0:
                        dve.wait_ge(ln_step, 9 * s)
                    for j in range(T):
                        dve.wait_ge(x_in[n % 2][j], DMA_INC // 2 * (s + (2 - n % 2)))
                        nc.vector.bn_stats(stats[:, j, :], x[j][:, :]).then_inc(ln_step, 1)

                def variance(s):
                    for j in range(T):
                        nc.vector.bn_aggr(mean_var[:, j, :], stats[:, j, :]).then_inc(ln_step, 1)
                    dve.wait_ge(ln_step, 9 * s + 2 * T)
                    nc.vector.tensor_scalar(var_eps[:, :], mean_var[:, :, 1], EPS, None, ALU.add).then_inc(ln_step, 1)

                def normalise(s, n):
                    dve.wait_ge(rstd_ready, s + 1)
                    if n > 0:
                        dve.wait_ge(xt_psum, C * s)
                    for j in range(T):
                        nc.vector.tensor_scalar(xn[:, j, :], x_sb[n % 2][j][:, :], mean_var[:, j, 0:1],
                                                rstd[:, j:j + 1], ALU.subtract, ALU.mult).then_inc(xn_ready, 1)

                def square_lo(s, c):
                    dve.wait_ge(act_hi, C * s + c + 1)
                    nc.vector.tensor_tensor(kact_lo[:, c, :], kact[:, c, :], kact_hi[:, c, :].bitcast(F32),
                                            ALU.subtract).then_inc(act_lo, 1)

                def mix(s, name, c, done):
                    m = mixed[name][:, c, :].rearrange("p (b t) -> p b t", b=2)
                    nc.vector.scalar_tensor_tensor(out=m, in0=xt[:, c, :, 0:S], scalar=one_minus_mu[name][:, c:c + 1],
                                                   in1=m, op0=ALU.mult, op1=ALU.add).then_inc(done, 1)

                def mix_k(s, n, c):
                    dve.wait_ge(xt_ready, C * s + c + 1)
                    mix(s, "k", c, k_mixed)
                    mix(s, "r", c, r_mixed)
                    if n > 0 and c == 0:
                        dve.wait_ge(k_psum, C * s)
                    dve.wait_ge(k_mixed, C * s + c + 1)
                    nc.vector.tensor_copy(m_hi["k"][:, c, :], mixed["k"][:, c, :]).then_inc(k_hi, 1)
                    dve.wait_ge(k_hi, C * s + c + 1)
                    nc.vector.tensor_tensor(m_lo["k"][:, c, :], mixed["k"][:, c, :], m_hi["k"][:, c, :].bitcast(F32),
                                            ALU.subtract).then_inc(k_lo, 1)

                def mix_r_lo(s, n, c):
                    dve.wait_ge(r_hi, C * s + c + 1)
                    nc.vector.tensor_tensor(m_lo["r"][:, c, :], mixed["r"][:, c, :], m_hi["r"][:, c, :].bitcast(F32),
                                            ALU.subtract).then_inc(r_lo, 1)

                def product(s, j):
                    dve.wait_ge(tanh_ready, T * s + j + 1)
                    dve.wait_ge(v_psum, T * s + j + 1)
                    nc.vector.scalar_tensor_tensor(out=tanh_r[:, j, :], in0=tanh_r[:, j, :], scalar=1.0,
                                                   in1=kv_bank[j][:, :], op0=ALU.add, op1=ALU.mult)\
                        .then_inc(product_ready, 1)

                def step(s, n):
                    if has(n + 1):
                        statistics(s + 1, n + 1)
                        dve.wait_ge(ln_step, 9 * (s + 1) + T)
                        if n >= 0:
                            dve.wait_ge(xn_ready, T * (s + 1))
                    if has(n):
                        square_lo(s, 0)
                    if has(n + 1):
                        variance(s + 1)
                    if has(n):
                        square_lo(s, 1)
                    if has(n + 1):
                        normalise(s + 1, n + 1)
                    if has(n):
                        for c in range(2, C):
                            square_lo(s, c)
                    if has(n + 1):
                        for c in range(C):
                            mix_k(s + 1, n + 1, c)
                    for c in range(C):
                        if has(n + 1):
                            mix_r_lo(s + 1, n + 1, c)
                        if has(n):
                            product(s, c)

                run(dve, step)

            @block.tensor
            def _(pe):
                def keys(s, n, c):
                    if c == 0:
                        pe.wait_ge(k_lo, C * (s + 1))
                    if n > 0:
                        pe.wait_ge(product_ready, T * s - T + c + 1)
                    cols = slice(c * P, (c + 1) * P)
                    for i in range(C):
                        nc.tensor.matmul(kv_bank[c][:, :], w_hi["k"][:, i, cols], m_hi["k"][:, i, :],
                                         start=(i == 0), stop=False)
                        nc.tensor.matmul(kv_bank[c][:, :], w_hi["k"][:, i, cols], m_lo["k"][:, i, :],
                                         start=False, stop=False)
                        last = nc.tensor.matmul(kv_bank[c][:, :], w_lo["k"][:, i, cols], m_hi["k"][:, i, :],
                                                start=False, stop=(i == C - 1))
                    last.then_inc(k_psum, 1)

                def token_product(w, hi, lo, bank, j):
                    at = slice(j * P, (j + 1) * P)
                    for i in range(C):
                        nc.tensor.matmul(bank[:, :], hi[:, i, at], w_hi[w][:, i, :], start=(i == 0), stop=False)
                        nc.tensor.matmul(bank[:, :], hi[:, i, at], w_lo[w][:, i, :], start=False, stop=False)
                        last = nc.tensor.matmul(bank[:, :], lo[:, i, at], w_hi[w][:, i, :], start=False,
                                                stop=(i == C - 1))
                    return last

                def receptance(s, n, j):
                    if j == 0:
                        pe.wait_ge(r_lo, C * (s + 1))
                    if n > 0 or j >= 2:
                        pe.wait_ge(tanh_ready, T * s + j - 1)
                    token_product("r", m_hi["r"], m_lo["r"], r_bank[j % 2], j).then_inc(r_psum, 1)

                def values(s, n, j):
                    if j == 0:
                        pe.wait_ge(act_lo, C * (s + 1))
                    pe.wait_ge(relu_ready, C * s + j + 1)
                    token_product("v", kact_hi, kact_lo, kv_bank[j], j).then_inc(v_psum, 1)

                def transposes(s, n, c):
                    if c == 0:
                        pe.wait_ge(xn_ready, T * (s + 1))
                    if n > 0 or c >= 2:
                        pe.wait_ge(xt_ready, C * s + c - 1)
                    for j in range(T):
                        last = nc.tensor.transpose(t_bank[c % 2][:, j * P:(j + 1) * P], xn[:, j, c * P:(c + 1) * P],
                                                   eye_sb[:, :])
                    last.then_inc(xt_psum, 1)

                def step(s, n):
                    if has(n):
                        for c in range(C):
                            keys(s, n, c)
                    for j in range(C):
                        if has(n):
                            receptance(s, n, j)
                        if has(n + 1):
                            transposes(s + 1, n + 1, j)
                    if has(n):
                        for j in range(T):
                            values(s, n, j)

                run(pe, step)


def build(nc, x, ctx_t, g_a, wq_t, bq, wk_t, bk, wv_t, bv, wo_t, bo, g_f, fr_t, fk_t, fv_t, mu_r, mu_k, eye, x1, out):
    with ExitStack() as scope:
        psum = [scope.enter_context(nc.psum_tensor(f"bank{i}", [P, BANK], F32)) for i in range(8)]
        attention_pass(nc, psum, x, ctx_t, g_a, wq_t, bq, wk_t, bk, wv_t, bv, wo_t, bo, eye, x1)
        channel_mix_pass(nc, psum, x1, g_f, fr_t, fk_t, fv_t, mu_r, mu_k, eye, out)


def kernel(**inputs):
    import numpy as _np
    import concourse.bacc as _bacc
    from concourse import mybir as _mybir
    from concourse.bass_utils import run_bass_kernel_spmd as _run

    a = {n: _np.asarray(v) for n, v in inputs.items()}
    B, S, D = a["x"].shape

    def t(w):
        return _np.ascontiguousarray(w.T)

    def column(v):
        return _np.ascontiguousarray(v.reshape(D // P, P).T)

    def everywhere(v):
        return _np.ascontiguousarray(_np.broadcast_to(v.reshape(1, 1), (P, 1)))

    data = dict(
        x=a["x"], ctx_t=_np.ascontiguousarray(a["ctx_1024"].transpose(0, 2, 1)), g_a=everywhere(a["g_xattn"]),
        wq_t=t(a["L0_xattn_Wq"]), bq=column(a["L0_xattn_bq"]), wk_t=t(a["L0_xattn_Wk"]), bk=column(a["L0_xattn_bk"]),
        wv_t=t(a["L0_xattn_Wv"]), bv=column(a["L0_xattn_bv"]), wo_t=t(a["L0_xattn_Wo"]),
        bo=_np.ascontiguousarray(a["L0_xattn_bo"].reshape(1, D)), g_f=everywhere(a["g_ffn"]),
        fr_t=t(a["L0_ffn_W_r"]), fk_t=t(a["L0_ffn_W_k"]), fv_t=t(a["L0_ffn_W_v"]),
        mu_r=column(a["L0_ffn_mu_r"]), mu_k=column(a["L0_ffn_mu_k"]), eye=_np.eye(P, dtype=_np.float32),
    )
    nc = _bacc.Bacc("TRN2", target_bir_lowering=False, num_devices=1)
    arrays, args = {}, {}
    for name, v in data.items():
        v = _np.ascontiguousarray(v)
        arrays[f"in_{name}"] = v
        args[name] = nc.dram_tensor(f"in_{name}", v.shape, _mybir.dt.from_np(v.dtype), kind="ExternalInput").ap()
    args["x1"] = nc.dram_tensor("x1_dram", (B, S, D), F32, kind="Internal").ap()
    args["out"] = nc.dram_tensor("out_0", (B, S, D), F32, kind="ExternalOutput").ap()
    build(nc, **args)
    r = _run(nc, [arrays], core_ids=[0])
    return r.results[0]["out_0"]
```

```python
import math
from contextlib import ExitStack

import concourse.bass as bass
from concourse import mybir


P = 128
BANK = 512
EPS = 1e-5
DMA_INC = 16

ALU = mybir.AluOpType
ACT = mybir.ActivationFunctionType
AX = mybir.AxisListType
F32 = mybir.dt.float32
F32R = mybir.dt.float32r
F16 = mybir.dt.float16
BF16 = mybir.dt.bfloat16


def attention_pass(nc, psum, x, ctx_t, g, wq_t, bq, wk_t, bk, wv_t, bv, wo_t, bo, eye, parts_dram, x1):
    B, S, D = x.shape
    C = D // P
    HD = 32
    H = D // HD
    HC = P // HD
    T = S // P
    SCALE = float(HD) ** -0.5
    VPARTS = 3
    VW = VPARTS * HD + 1
    KROWS = 3 * HD
    MROW = KROWS
    SROWS = KROWS + 2
    SHIFT = 12 * math.log(2.0) / SCALE
    PAIRS = C // 2
    HP = H // PAIRS
    STACK = DMA_INC * 3
    HG = 2
    G = H // HG
    assert S == 2 * P and T == 2 and D == BANK and C == 4

    with ExitStack() as weights_scope:
        def wsb(name, shape, dt):
            return weights_scope.enter_context(nc.sbuf_tensor(name, shape, dt))

        w_hi = {n: wsb(f"w{n}_hi", [P, C, D], F32R) for n in "qkvo"}
        w_lo = {n: wsb(f"w{n}_lo", [P, C, D], F32R) for n in "qkvo"}
        eye_sb = wsb("eye_sb", [P, P], F32)
        bq_sb = wsb("bq_sb", [P, C], F32)
        bk_sb = wsb("bk_sb", [P, C], F32)
        out_bias = wsb("out_bias", [P, D], F32)
        minus_half = wsb("minus_half", [P, T], F32)

        with ExitStack() as scope:
            def sb(name, shape, dt):
                return scope.enter_context(nc.sbuf_tensor(name, shape, dt))

            def sem(name):
                return scope.enter_context(nc.semaphore(name))

            raw = {n: sb(f"w{n}_raw", [P, C, D], F32) for n in "qkvo"}
            gate = sb("gate_a", [P, 1], F32)
            bv_sb = sb("bv_sb", [P, C], F32)
            bo_sb = sb("bo_sb", [1, D], F32)
            bias_row = sb("bias_row", [1, D], F32)
            ones_row = sb("ones_row", [1, P], F32)
            w_in = {n: sem(f"w{n}_in") for n in "qkvo"}
            small_in = sem("small_in_a")
            gate_ready = sem("gate_ready_a")
            gated = sem("gated_a")
            hi_ready = sem("w_hi_ready_a")
            lo_ready = sem("w_lo_ready_a")
            ones_ready = sem("ones_ready_a")
            bias_psum = sem("bias_psum")
            bias_ready = sem("bias_ready")
            source = dict(q=wq_t, k=wk_t, v=wv_t, o=wo_t)

            with nc.Block() as block:
                @block.sync
                def _(sp):
                    smalls = [(gate[:, :], g), (bq_sb[:, :], bq), (bk_sb[:, :], bk), (bv_sb[:, :], bv),
                              (bo_sb[:, :], bo), (eye_sb[:, :], eye)]
                    for dst, src in smalls:
                        sp.dma_start(dst, src).then_inc(small_in, DMA_INC)
                    for n in "oqkv":
                        sp.dma_start(raw[n][:, :, :], source[n].rearrange("(c p) n -> p c n", p=P)).then_inc(w_in[n], DMA_INC)

                @block.scalar
                def _(act):
                    act.wait_ge(small_in, 6 * DMA_INC)
                    nc.scalar.activation(gate[:, :], gate[:, :], ACT.Tanh).then_inc(gate_ready, 1)
                    for i, n in enumerate("qkvo"):
                        if n == "o":
                            act.wait_ge(gated, 1)
                        else:
                            act.wait_ge(w_in[n], DMA_INC)
                        nc.scalar.activation(w_hi[n][:, :, :], raw[n][:, :, :], ACT.Copy).then_inc(hi_ready, 1)

                @block.vector
                def _(dve):
                    nc.vector.memset(ones_row[:, :], 1.0).then_inc(ones_ready, 1)
                    nc.vector.memset(minus_half[:, :], -0.5).then_inc(ones_ready, 1)
                    dve.wait_ge(gate_ready, 1)
                    dve.wait_ge(w_in["o"], DMA_INC)
                    nc.vector.tensor_scalar(raw["o"][:, :, :], raw["o"][:, :, :], gate[:, 0:1], None,
                                            ALU.mult).then_inc(gated, 1)
                    for i, n in enumerate("qkvo"):
                        dve.wait_ge(hi_ready, i + 1)
                        nc.vector.tensor_tensor(w_lo[n][:, :, :], raw[n][:, :, :], w_hi[n][:, :, :].bitcast(F32),
                                                ALU.subtract).then_inc(lo_ready, 1)
                    dve.wait_ge(bias_psum, 1)
                    nc.vector.scalar_tensor_tensor(out=bias_row[:, :], in0=bo_sb[:, :], scalar=gate[0:1, 0:1],
                                                   in1=psum[0][0:1, :], op0=ALU.mult, op1=ALU.add).then_inc(bias_ready, 1)
                    dve.wait_ge(bias_psum, 2)
                    nc.vector.tensor_copy(out_bias[:, :], psum[1][:, :]).then_inc(bias_ready, 1)
                    dve.wait_ge(lo_ready, 4)

                @block.tensor
                def _(pe):
                    pe.wait_ge(gated, 1)
                    for c in range(C):
                        last = nc.tensor.matmul(psum[0][0:1, :], bv_sb[:, c:c + 1], raw["o"][:, c, :],
                                                start=(c == 0), stop=(c == C - 1))
                    last.then_inc(bias_psum, 1)
                    pe.wait_ge(ones_ready, 2)
                    pe.wait_ge(bias_ready, 1)
                    nc.tensor.matmul(psum[1][:, :], ones_row[:, :], bias_row[:, :],
                                     start=True, stop=True).then_inc(bias_psum, 1)

        with ExitStack() as scope:
            def sb(name, shape, dt):
                return scope.enter_context(nc.sbuf_tensor(name, shape, dt))

            def sem(name):
                return scope.enter_context(nc.semaphore(name))

            x_sb = [sb(f"x_sb{j}", [P, D], F32) for j in range(T)]
            stats = sb("stats_a", [P, T, 6], F32)
            mean_var = sb("mean_var_a", [P, T, 2], F32)
            var_eps = sb("var_eps_a", [P, T], F32)
            rstd = sb("rstd_a", [P, T], F32)
            xn_hi = sb("xn_hi", [P, C, S], F32R)
            xn_lo = sb("xn_lo", [P, C, S], F32R)
            ctx_raw = sb("ctx_raw", [P, C, S], F32)
            ctx_hi = [sb(f"ctx_hi{i}", [P, C, S], F32R) for i in range(2)]
            ctx_lo = [sb(f"ctx_lo{i}", [P, C, S], F32R) for i in range(2)]
            parts = sb("parts", [P, C, 2, S], F32R)
            q_stack = [sb(f"q_stack{i}", [P, H, S], F32R) for i in range(2)]
            k_stack = [sb(f"k_stack{i}", [P, H, S], F32R) for i in range(2)]
            v_sb = [sb(f"v_sb{i}", [P, T, H, VW], BF16) for i in range(2)]
            row_max = sb("row_max", [P, H, T], F32)
            max_row = sb("max_row", [H * T, 2, P], F32R)
            probs = sb("probs", [P, T, S], F32)
            probs_hi = [sb(f"probs_hi{i}", [P, T, S], F16) for i in range(2)]
            probs_lo = [sb(f"probs_lo{i}", [P, T, S], F16) for i in range(2)]
            inv_sum = sb("inv_sum", [P, HG, T], F32)
            o_sum = sb("o_sum", [P, HG, T, HD], F32)
            o_first = [sb(f"o_first{i}", [P, T, HC, HD], F32) for i in range(2)]
            o_rest = [sb(f"o_rest{c}", [P, T, HC, HD], F32) for c in range(1, C)]
            o_hi = [sb(f"o_hi{j}", [P, C, P], F32R) for j in range(T)]
            o_lo = [sb(f"o_lo{j}", [P, C, P], F32R) for j in range(T)]
            res = [sb(f"res{j}", [P, D], F32) for j in range(T)]

            acc = psum[0:2]
            s_bank = psum[2:4]
            st_bank = psum[4:6]
            pv_bank = psum[6:8]

            consts = sem("consts")
            x_in = [sem(f"x_in{j}") for j in range(T)]
            ln_step = sem("ln_step")
            rstd_ready = sem("rstd_ready")
            xn_ready = sem("xn_ready")
            xt_psum = sem("xt_psum")
            xt_hi = sem("xt_hi")
            xt_lo = sem("xt_lo")
            ctx_in = sem("ctx_in")
            ctx_hi_ready = sem("ctx_hi_ready")
            ctx_lo_ready = sem("ctx_lo_ready")
            k_psum = sem("k_psum")
            k_hi_ready = sem("k_hi_ready")
            k_lo_ready = sem("k_lo_ready")
            q_psum = sem("q_psum")
            q_hi_ready = sem("q_hi_ready")
            q_lo_ready = sem("q_lo_ready")
            k_saved = [sem(f"k_saved{i}") for i in range(PAIRS)]
            q_saved = [sem(f"q_saved{i}") for i in range(PAIRS)]
            k_stacked = [sem(f"k_stacked{i}") for i in range(PAIRS)]
            q_stacked = [sem(f"q_stacked{i}") for i in range(PAIRS)]
            v_psum = sem("v_psum")
            v1_ready = sem("v1_ready")
            v_rest = sem("v_rest")
            v2_ready = sem("v2_ready")
            v_ready = sem("v_ready")
            s_psum = sem("s_psum")
            max_ready = sem("max_ready")
            max_psum = sem("max_psum")
            max_copied = sem("max_copied")
            max_stacked = sem("max_stacked")
            st_psum = sem("st_psum")
            probs_ready = sem("probs_ready")
            probs_lo_ready = sem("probs_lo_ready")
            pv_psum = sem("pv_psum")
            pv_read = sem("pv_read")
            o_ready = sem("o_ready")
            ot_psum = sem("ot_psum")
            ot_hi = sem("ot_hi")
            ot_lo = sem("ot_lo")
            o_psum = sem("o_psum")
            res_in = [sem(f"res_in{j}") for j in range(T)]
            res_biased = sem("res_biased")
            x1_ready = sem("x1_ready")
            x1_out = [sem(f"x1_out{j}") for j in range(T)]

            SCORE_SLOTS = (1, 1, 1, 2, 1, 2, 1, 2, 1, 2, 1, 1)
            assert sum(SCORE_SLOTS) == H
            FIRST_STEADY = 4
            LAST_STEADY = B - 2
            assert (LAST_STEADY - FIRST_STEADY) % 2 == 0

            def run(eng, step):
                for s in range(-1, FIRST_STEADY):
                    step(s, s)
                with eng.Fori(0, (LAST_STEADY - FIRST_STEADY) // 2) as i:
                    for j in range(2):
                        step(2 * i + (FIRST_STEADY + j), FIRST_STEADY + j)
                for s in range(LAST_STEADY, B + 4):
                    step(s, s)

            def has(n):
                return 0 <= n < B

            def scored(k):
                return range(sum(SCORE_SLOTS[:k]), sum(SCORE_SLOTS[:k + 1])) if k < len(SCORE_SLOTS) else range(0)

            def o_chunk(n, c):
                return o_first[n % 2] if c == 0 else o_rest[c - 1]

            block = scope.enter_context(nc.Block())

            @block.sync
            def _(sp):
                def save(b, n, pair, which, ready, saved):
                    sp.wait_ge(ready, 2 * b + pair + 1)
                    cs = slice(2 * pair, 2 * pair + 2)
                    dst = parts_dram[which, n % 2, :, :, :].rearrange("(c p) a t -> p c (a t)", p=P)
                    sp.dma_start(dst[:, cs, :], parts[:, cs, :, :].rearrange("p c a t -> p c (a t)").bitcast(F32)).then_inc(saved[pair], DMA_INC)

                def stack(b, n, pair, which, dst, order, saved, stacked):
                    sp.wait_ge(saved[pair], DMA_INC * (b + 1))
                    hs = slice(HP * pair, HP * pair + HP)
                    for i, part in enumerate(order):
                        src = parts_dram[which, n % 2, :, part, :].rearrange("(h p) t -> p h t", p=HD)
                        sp.dma_start(dst[n % 2][HD * i:HD * i + HD, hs, :].bitcast(F32), src[:, hs, :])\
                            .then_inc(stacked[pair], DMA_INC)

                def stack_k(b, n, pair, through):
                    if n >= 2 and not through:
                        sp.wait_ge(st_psum, H * (b - 2) + (pair + 1) * HP)
                    stack(b, n, pair, 0, k_stack, (0, 1, 0), k_saved, k_stacked)

                def stack_q(b, n, pair):
                    stack(b, n, pair, 1, q_stack, (0, 0, 1), q_saved, q_stacked)

                def store(b, j):
                    sp.wait_ge(x1_ready, 2 * b + j + 1)
                    sp.dma_start(x1[b, j * P:(j + 1) * P, :], res[j][:, :]).then_inc(x1_out[j], DMA_INC)

                def step(s, n):
                    if has(n - 4):
                        store(s - 4, 1)
                    if has(n - 1):
                        stack_k(s - 1, n - 1, 1, has(n - 4))
                        stack_q(s - 1, n - 1, 1)
                    if has(n + 1):
                        for j in range(T):
                            if n >= 0:
                                sp.wait_ge(xt_psum, 2 * s + j + 1)
                            sp.dma_start(x_sb[j][:, :], x[s + 1, j * P:(j + 1) * P, :]).then_inc(x_in[j], DMA_INC)
                        if n >= 0:
                            sp.wait_ge(ctx_lo_ready, 2 * (s + 1))
                        sp.dma_start(ctx_raw[:, :, :], ctx_t[s + 1, :, :].rearrange("(c p) t -> p c t", p=P))\
                            .then_inc(ctx_in, DMA_INC)
                    if has(n):
                        save(s, n, 0, 0, k_lo_ready, k_saved)
                        save(s, n, 1, 0, k_lo_ready, k_saved)
                    if has(n - 3):
                        for j in range(T):
                            if has(n - 1):
                                sp.wait_ge(v_ready, 2 * (s - 1) + j + 1)
                            elif n >= 4:
                                sp.wait_ge(x1_out[j], DMA_INC * (s - 3))
                            sp.dma_start(res[j][:, :], x[s - 3, j * P:(j + 1) * P, :]).then_inc(res_in[j], DMA_INC)
                    if has(n):
                        stack_k(s, n, 0, has(n - 3) and has(n - 1))
                        save(s, n, 0, 1, q_lo_ready, q_saved)
                        stack_q(s, n, 0)
                        save(s, n, 1, 1, q_lo_ready, q_saved)
                    if has(n - 3):
                        store(s - 3, 0)

                run(sp, step)
                for j in range(T):
                    sp.wait_ge(x1_out[j], DMA_INC * B)

            @block.gpsimd
            def _(pool):
                def probs_rest(b, n, u):
                    pool.wait_ge(probs_ready, H * b + u + 1)
                    nc.gpsimd.tensor_tensor(probs_lo[u % 2][:, :, :], probs[:, :, :], probs_hi[u % 2][:, :, :],
                                            ALU.subtract).then_inc(probs_lo_ready, 1)

                def context_lo(b, n, half):
                    pool.wait_ge(ctx_hi_ready, b + 1)
                    cs = slice(half * C // 2, (half + 1) * C // 2)
                    nc.gpsimd.tensor_tensor(ctx_lo[n % 2][:, cs, :], ctx_raw[:, cs, :],
                                            ctx_hi[n % 2][:, cs, :].bitcast(F32), ALU.subtract).then_inc(ctx_lo_ready, 1)

                def bias(b, j):
                    pool.wait_ge(res_in[j], DMA_INC * (b + 1))
                    nc.gpsimd.tensor_tensor(res[j][:, :], res[j][:, :], out_bias[:, :], ALU.add).then_inc(res_biased, 1)

                def step(s, n):
                    for k in range(H):
                        if has(n - 2):
                            probs_rest(s - 2, n - 2, k)
                        if k in (10, 11) and has(n + 1):
                            context_lo(s + 1, n + 1, k - 10)
                        if k in (9, 12) and has(n - 3):
                            bias(s - 3, (k - 9) // 3)
                        if k == 14 and has(n + 1):
                            pool.wait_ge(ln_step, 5 * (s + 2))
                            nc.gpsimd.tensor_tensor(rstd[:, :], var_eps[:, :], minus_half[:, :], ALU.pow)\
                                .then_inc(rstd_ready, 1)

                run(pool, step)

            @block.scalar
            def _(act):
                def exp_hi(b, n, u):
                    act.wait_ge(st_psum, H * b + u + 1)
                    if n > 0 or u >= 2:
                        act.wait_ge(pv_psum, H * b + u - 1)
                    nc.scalar.activation(probs_hi[u % 2][:, :, :].rearrange("p a t -> p (a t)"), st_bank[u % 2][:, :],
                                         ACT.Exp, scale=SCALE)

                def exp(b, n, u):
                    if n > 0 or u > 0:
                        act.wait_ge(probs_lo_ready, H * b + u)
                    nc.scalar.activation(probs[:, :, :].rearrange("p a t -> p (a t)"), st_bank[u % 2][:, :],
                                         ACT.Exp, scale=SCALE).then_inc(probs_ready, 1)

                def transposed_hi(b, n, j):
                    act.wait_ge(xt_psum, 2 * b + j + 1)
                    if n > 0:
                        act.wait_ge(q_psum, 2 * b)
                    nc.scalar.activation(xn_hi[:, :, j * P:(j + 1) * P], acc[1 - j][:, :].rearrange("p (c t) -> p c t", c=C),
                                         ACT.Copy).then_inc(xt_hi, 1)

                def projected_hi(b, n, pair, bias, bank, done, ready):
                    act.wait_ge(done, 2 * b + pair + 1)
                    if done is q_psum:
                        act.wait_ge(k_saved[pair], DMA_INC * (b + 1))
                    elif n > 0:
                        act.wait_ge(q_saved[pair], DMA_INC * b)
                    for c in range(2 * pair, 2 * pair + 2):
                        at = (c % 2) * S
                        last = nc.scalar.activation(parts[:, c, 0, :], bank[:, at:at + S], ACT.Identity, bias=bias[:, c:c + 1])
                    last.then_inc(ready, 1)

                def value_part(n, j, i):
                    return v_sb[n % 2][:, j, :, i * HD:(i + 1) * HD]

                def values_1(b, n, j):
                    act.wait_ge(v_psum, 2 * b + j + 1)
                    if n >= 2:
                        act.wait_ge(pv_psum, H * (b - 1))
                    nc.scalar.activation(value_part(n, j, 0), acc[j][:, :].rearrange("p (h d) -> p h d", h=H),
                                         ACT.Copy).then_inc(v1_ready, 1)

                def values_2(b, n, j):
                    act.wait_ge(v_rest, 2 * b + j + 1)
                    nc.scalar.activation(value_part(n, j, 1), res[j][:, :].rearrange("p (h d) -> p h d", h=H),
                                         ACT.Copy).then_inc(v2_ready, 1)

                def output_hi(b, n, j):
                    act.wait_ge(ot_psum, 2 * b + j + 1)
                    if n > 0:
                        act.wait_ge(o_psum, 2 * b + j - 1)
                    nc.scalar.activation(o_hi[j][:, :, :], acc[1 - j][:, :].rearrange("p (c t) -> p c t", c=C),
                                         ACT.Copy).then_inc(ot_hi, 1)

                def step(s, n):
                    for k in range(H):
                        if k in (2, 4) and has(n):
                            projected_hi(s, n, k // 2 - 1, bk_sb, acc[k // 2 - 1], k_psum, k_hi_ready)
                        if k in (6, 8) and has(n - 1):
                            values_1(s - 1, n - 1, (k - 6) // 2)
                        if k in (10, 12) and has(n):
                            i = (k - 10) // 2
                            projected_hi(s, n, i, bq_sb, acc[i], q_psum, q_hi_ready)
                        if has(n - 2):
                            exp_hi(s - 2, n - 2, k)
                        if k in (1, 3) and has(n):
                            transposed_hi(s, n, k // 2)
                        if k in (5, 7) and has(n - 3):
                            output_hi(s - 3, n - 3, (k - 5) // 2)
                        if k in (7, 9) and has(n - 1):
                            values_2(s - 1, n - 1, (k - 7) // 2)
                        if has(n - 2):
                            exp(s - 2, n - 2, k)
                        if k == 9 and has(n + 1):
                            act.wait_ge(ctx_in, DMA_INC * (s + 2))
                            if n >= 1:
                                act.wait_ge(v_psum, 2 * s)
                            nc.scalar.activation(ctx_hi[(n + 1) % 2][:, :, :], ctx_raw[:, :, :], ACT.Copy)\
                                .then_inc(ctx_hi_ready, 1)
                        if k == 13 and has(n - 1):
                            act.wait_ge(max_copied, 2 * s)
                            for i in range(2):
                                row = q_stack[(n - 1) % 2][MROW + i:MROW + i + 1, :, :]
                                act.dma_start(row.rearrange("o h (j t) -> o (h j) t", j=T).bitcast(F32),
                                              max_row[:, i, :].bitcast(F32)).then_inc(max_stacked, DMA_INC)

                run(act, step)

            @block.vector
            def _(dve):
                for i in range(2):
                    nc.vector.memset(v_sb[i][:, :, :, VW - 1:VW], 1.0).then_inc(consts, 1)
                    nc.vector.memset(k_stack[i][MROW:SROWS, :, :].bitcast(F32), -1.0).then_inc(consts, 1)

                def residual(b, j):
                    dve.wait_ge(o_psum, 2 * b + j + 1)
                    dve.wait_ge(res_biased, 2 * b + j + 1)
                    nc.vector.tensor_tensor(res[j][:, :], acc[j][:, :], res[j][:, :], ALU.add).then_inc(x1_ready, 1)

                def normalise(b, n, grp):
                    bank = pv_bank[grp % 2][:, 0:HG * T * VW].rearrange("p (u v) -> p u v", v=VW)
                    chunk, h = grp * HG // HC, grp * HG % HC
                    out = o_chunk(n, chunk)[:, :, h:h + HG, :].rearrange("p j h d -> p h j d")
                    dve.wait_ge(pv_psum, H * b + HG * (grp + 1))
                    if n > 0 or grp > 0:
                        dve.wait_ge(o_ready, G * b + grp)
                    nc.vector.reciprocal(inv_sum[:, :, :].rearrange("p h j -> p (h j)"), bank[:, :, VW - 1]).then_inc(pv_read, 1)
                    nc.vector.tensor_reduce(o_sum[:, :, :, :].rearrange("p h j d -> p (h j) d"),
                                            bank[:, :, 0:VW - 1].rearrange("p u (i d) -> p u d i", i=VPARTS),
                                            AX.X, ALU.add).then_inc(pv_read, 1)
                    if grp == 0 and n >= 2:
                        dve.wait_ge(ot_psum, 2 * (b - 1))
                    elif h == 0 and chunk > 0 and n > 0:
                        dve.wait_ge(ot_psum, 2 * b)
                    dve.wait_ge(pv_read, 2 * (G * b + grp + 1))
                    nc.vector.tensor_tensor(out, o_sum[:, :, :, :],
                                            inv_sum[:, :, :].unsqueeze(3).to_broadcast([P, HG, T, HD]),
                                            ALU.mult).then_inc(o_ready, 1)

                def values_rest(b, n, j):
                    dve.wait_ge(v1_ready, 2 * b + j + 1)
                    if n > 0:
                        dve.wait_ge(v_ready, 2 * b + j - 1)
                    if n >= 3:
                        dve.wait_ge(x1_out[j], DMA_INC * (b - 2))
                    part = v_sb[n % 2][:, j, :, 0:HD]
                    nc.vector.tensor_tensor(res[j][:, :].rearrange("p (h d) -> p h d", h=H),
                                            acc[j][:, :].rearrange("p (h d) -> p h d", h=H), part,
                                            ALU.subtract).then_inc(v_rest, 1)

                def values_3(b, n, j):
                    dve.wait_ge(v2_ready, 2 * b + j + 1)
                    v = v_sb[n % 2][:, j, :, :]
                    nc.vector.tensor_tensor(v[:, :, 2 * HD:3 * HD], res[j][:, :].rearrange("p (h d) -> p h d", h=H),
                                            v[:, :, HD:2 * HD], ALU.subtract).then_inc(v_ready, 1)

                def transposed_lo(b, j):
                    dve.wait_ge(xt_hi, 2 * b + j + 1)
                    at = slice(j * P, (j + 1) * P)
                    nc.vector.tensor_tensor(xn_lo[:, :, at], acc[1 - j][:, :].rearrange("p (c t) -> p c t", c=C),
                                            xn_hi[:, :, at].bitcast(F32), ALU.subtract).then_inc(xt_lo, 1)

                def projected_lo(b, pair, bias, bank, hi_ready, lo_ready):
                    dve.wait_ge(hi_ready, 2 * b + pair + 1)
                    for c in range(2 * pair, 2 * pair + 2):
                        at = (c % 2) * S
                        last = nc.vector.scalar_tensor_tensor(out=parts[:, c, 1, :], in0=bank[:, at:at + S],
                                                              scalar=bias[:, c:c + 1], in1=parts[:, c, 0, :].bitcast(F32),
                                                              op0=ALU.add, op1=ALU.subtract)
                    last.then_inc(lo_ready, 1)

                def output_lo(b, j):
                    dve.wait_ge(ot_hi, 2 * b + j + 1)
                    nc.vector.tensor_tensor(o_lo[j][:, :, :], acc[1 - j][:, :].rearrange("p (c t) -> p c t", c=C),
                                            o_hi[j][:, :, :].bitcast(F32), ALU.subtract).then_inc(ot_lo, 1)

                def maximum(b, n, u):
                    dve.wait_ge(s_psum, H * b + u + 1)
                    if n > 0 and u == 0:
                        dve.wait_ge(max_psum, b)
                    nc.vector.tensor_reduce(row_max[:, u, :], s_bank[u % 2][:, :].rearrange("p (j t) -> p j t", j=T),
                                            AX.X, ALU.max).then_inc(max_ready, 1)

                def statistics(b, n):
                    if n > 0:
                        dve.wait_ge(ln_step, 5 * b)
                    for j in range(T):
                        dve.wait_ge(x_in[j], DMA_INC * (b + 1))
                        nc.vector.bn_stats(stats[:, j, :], x_sb[j][:, :]).then_inc(ln_step, 1)

                def variance(b):
                    for j in range(T):
                        nc.vector.bn_aggr(mean_var[:, j, :], stats[:, j, :]).then_inc(ln_step, 1)
                    dve.wait_ge(ln_step, 5 * b + 2 * T)
                    nc.vector.tensor_scalar(var_eps[:, :], mean_var[:, :, 1], EPS, None, ALU.add).then_inc(ln_step, 1)

                def layer_norm(b):
                    dve.wait_ge(rstd_ready, b + 1)
                    for j in range(T):
                        nc.vector.tensor_scalar(x_sb[j][:, :], x_sb[j][:, :], mean_var[:, j, 0:1], rstd[:, j:j + 1],
                                                ALU.subtract, ALU.mult).then_inc(xn_ready, 1)

                def step(s, n):
                    for k in range(H):
                        if k == 0 and has(n - 4):
                            residual(s - 4, 1)
                        if k == 13 and has(n - 1):
                            dve.wait_ge(max_psum, s)
                            if n >= 2:
                                dve.wait_ge(max_stacked, 2 * DMA_INC * (s - 1))
                            nc.vector.tensor_scalar(max_row[:, 0, :], s_bank[0][0:H * T, 0:P], -SHIFT, None,
                                                    ALU.add).then_inc(max_copied, 1)
                            dve.wait_ge(max_copied, 2 * s - 1)
                            nc.vector.scalar_tensor_tensor(out=max_row[:, 1, :], in0=s_bank[0][0:H * T, 0:P],
                                                           scalar=-SHIFT, in1=max_row[:, 0, :].bitcast(F32),
                                                           op0=ALU.add, op1=ALU.subtract).then_inc(max_copied, 1)
                        if k in (1, 3) and has(n):
                            transposed_lo(s, k // 2)
                        if k in (2, 4) and has(n):
                            i = k // 2 - 1
                            projected_lo(s, i, bk_sb, acc[i], k_hi_ready, k_lo_ready)
                        if k in (6, 8) and has(n - 1):
                            values_rest(s - 1, n - 1, (k - 6) // 2)
                        if k in (5, 7) and has(n - 3):
                            output_lo(s - 3, (k - 5) // 2)
                        if k in (10, 12) and has(n):
                            i = (k - 10) // 2
                            projected_lo(s, i, bq_sb, acc[i], q_hi_ready, q_lo_ready)
                        for u in scored(k) if has(n - 1) else ():
                            maximum(s - 1, n - 1, u)
                        if k == 12 and has(n + 1):
                            dve.wait_ge(ln_step, 5 * (s + 1) + T)
                            if n >= 0:
                                dve.wait_ge(xn_ready, 2 * (s + 1))
                        if k in (0, 2) and has(n - 3):
                            normalise(s - 3, n - 3, G - 2 + k // 2)
                        if 4 <= k and k % 2 == 0 and has(n - 2):
                            normalise(s - 2, n - 2, k // 2 - 2)
                        if k in (7, 9) and has(n - 1):
                            values_3(s - 1, n - 1, (k - 7) // 2)
                        if k == 11 and has(n + 1):
                            statistics(s + 1, n + 1)
                        if k == 12 and has(n + 1):
                            variance(s + 1)
                        if k == 15 and has(n + 1):
                            layer_norm(s + 1)
                        if k == 14 and has(n - 3):
                            residual(s - 3, 0)

                run(dve, step)

            @block.tensor
            def _(pe):
                def scores_t(b, n, u):
                    if u == 0:
                        pe.wait_ge(max_stacked, 2 * DMA_INC * (b + 1))
                    if n > 0 or u >= 2:
                        pe.wait_ge(probs_ready, H * b + u - 1)
                    for t in range(T):
                        last = nc.tensor.matmul(st_bank[u % 2][:, t * S:(t + 1) * S],
                                                k_stack[n % 2][0:SROWS, u, t * P:(t + 1) * P],
                                                q_stack[n % 2][0:SROWS, u, :], start=True, stop=True)
                    last.then_inc(st_psum, 1)

                def weighted(b, n, u):
                    grp = u // HG
                    if u == 0:
                        pe.wait_ge(v_ready, 2 * b + 2)
                    if u % HG == 0 and (n > 0 or grp >= 2):
                        pe.wait_ge(pv_read, 2 * (G * b + grp - 1))
                    pe.wait_ge(probs_lo_ready, H * b + u + 1)
                    for j in range(T):
                        at = ((u % HG) * T + j) * VW
                        out = pv_bank[grp % 2][:, at:at + VW]
                        cols = slice(j * P, (j + 1) * P)
                        for t in range(T):
                            v = v_sb[n % 2][:, t, u, :]
                            nc.tensor.matmul(out, probs_hi[u % 2][:, t, cols], v, start=(t == 0), stop=False)
                            last = nc.tensor.matmul(out, probs_lo[u % 2][:, t, cols], v, start=False, stop=(t == T - 1))
                    last.then_inc(pv_psum, 1)

                def scores(b, n, u):
                    if u == 0:
                        pe.wait_ge(k_stacked[0], STACK * (b + 1))
                        pe.wait_ge(q_stacked[0], STACK * (b + 1))
                        if n > 0:
                            pe.wait_ge(max_copied, 2 * b)
                    elif u == H // 2:
                        pe.wait_ge(k_stacked[1], STACK * (b + 1))
                        pe.wait_ge(q_stacked[1], STACK * (b + 1))
                    if n > 0 or u >= 2:
                        pe.wait_ge(max_ready, H * b + u - 1)
                    for j in range(T):
                        last = nc.tensor.matmul(s_bank[u % 2][:, j * S:(j + 1) * S],
                                                q_stack[n % 2][0:KROWS, u, j * P:(j + 1) * P],
                                                k_stack[n % 2][0:KROWS, u, :], start=True, stop=True)
                    last.then_inc(s_psum, 1)

                def maxima(b, n):
                    pe.wait_ge(max_ready, H * (b + 1))
                    nc.tensor.transpose(s_bank[0][0:H * T, 0:P], row_max[:, :, :].rearrange("p h j -> p (h j)"),
                                        eye_sb[:, :]).then_inc(max_psum, 1)

                def transpose_x(s, n, j):
                    if j == 0:
                        if has(n - 4):
                            pe.wait_ge(x1_ready, 2 * (s - 4) + 2)
                        elif n >= 1:
                            pe.wait_ge(q_lo_ready, 2 * s)
                    else:
                        pe.wait_ge(k_lo_ready, 2 * s + 1)
                    pe.wait_ge(xn_ready, 2 * s + j + 1)
                    for c in range(C):
                        last = nc.tensor.transpose(acc[1 - j][:, c * P:(c + 1) * P], x_sb[j][:, c * P:(c + 1) * P],
                                                   eye_sb[:, :])
                    last.then_inc(xt_psum, 1)

                def transposed_product(w, act_hi, act_lo, pair, bank, half):
                    c = 2 * pair + half
                    cols = slice(c * P, (c + 1) * P)
                    out = bank[:, half * S:(half + 1) * S]
                    for i in range(C):
                        nc.tensor.matmul(out, w_hi[w][:, i, cols], act_hi[:, i, :], start=(i == 0), stop=False)
                        nc.tensor.matmul(out, w_hi[w][:, i, cols], act_lo[:, i, :], start=False, stop=False)
                        last = nc.tensor.matmul(out, w_lo[w][:, i, cols], act_hi[:, i, :], start=False, stop=(i == C - 1))
                    return last

                def keys(s, n, pair, half):
                    if half == 0:
                        if pair == 0:
                            pe.wait_ge(ctx_lo_ready, 2 * (s + 1))
                            if has(n - 4):
                                pe.wait_ge(x1_ready, 2 * (s - 4) + 1)
                            elif n >= 1:
                                pe.wait_ge(q_lo_ready, 2 * s - 1)
                        else:
                            pe.wait_ge(xt_lo, 2 * s + 1)
                    last = transposed_product("k", ctx_hi[n % 2], ctx_lo[n % 2], pair, acc[pair], half)
                    if half == 1:
                        last.then_inc(k_psum, 1)

                def queries(s, n, pair, half):
                    if half == 0:
                        if pair == 0:
                            pe.wait_ge(xt_lo, 2 * s + 2)
                            if has(n - 3):
                                pe.wait_ge(ot_lo, 2 * (s - 3) + 2)
                            elif has(n - 1):
                                pe.wait_ge(v_rest, 2 * s - 1)
                        elif has(n - 1):
                            pe.wait_ge(v_rest, 2 * s)
                        else:
                            pe.wait_ge(k_lo_ready, 2 * s + 2)
                    last = transposed_product("q", xn_hi, xn_lo, pair, acc[pair], half)
                    if half == 1:
                        last.then_inc(q_psum, 1)

                def token_product(w, act_hi, act_lo, bank, half, start, stop):
                    for i in (2 * half, 2 * half + 1):
                        nc.tensor.matmul(bank[:, :], act_hi(i), w_hi[w][:, i, :], start=(start and i == 0), stop=False)
                        nc.tensor.matmul(bank[:, :], act_hi(i), w_lo[w][:, i, :], start=False, stop=False)
                        last = nc.tensor.matmul(bank[:, :], act_lo(i), w_hi[w][:, i, :], start=False,
                                                stop=(stop and i == C - 1))
                    return last

                def values(s, n, j, half):
                    if half == 0:
                        if j == 0:
                            if has(n):
                                pe.wait_ge(xt_lo, 2 * s + 2)
                            else:
                                pe.wait_ge(x1_ready, 2 * (s - 4) + 1)
                        elif has(n - 3):
                            pe.wait_ge(ot_lo, 2 * (s - 3) + 1)
                        else:
                            pe.wait_ge(k_lo_ready, 2 * s + 2)
                    par, at = (n - 1) % 2, slice(j * P, (j + 1) * P)
                    last = token_product("v", lambda i: ctx_hi[par][:, i, at], lambda i: ctx_lo[par][:, i, at],
                                         acc[j], half, True, True)
                    if half == 1:
                        last.then_inc(v_psum, 1)

                def transpose_o(s, n, j):
                    if j == 0:
                        if has(n):
                            pe.wait_ge(k_lo_ready, 2 * s + 2)
                        elif has(n - 4):
                            pe.wait_ge(x1_ready, 2 * (s - 4) + 2)
                        pe.wait_ge(o_ready, G * (s - 2))
                    elif has(n - 1):
                        pe.wait_ge(v_rest, 2 * s - 1)
                    elif has(n - 4):
                        pe.wait_ge(x1_ready, 2 * (s - 4) + 1)
                    for c in range(C):
                        last = nc.tensor.transpose(acc[1 - j][:, c * P:(c + 1) * P], o_chunk(n - 3, c)[:, j, :, :].rearrange("p h d -> p (h d)"),
                                                   eye_sb[:, :])
                    last.then_inc(ot_psum, 1)

                def output(s, n, j, half):
                    if half == 0:
                        pe.wait_ge(ot_lo, 2 * (s - 3) + (2 if j == 0 else 2))
                        if has(n):
                            pe.wait_ge(q_lo_ready, 2 * s + j + 1)
                        elif has(n - 1) and j == 1:
                            pe.wait_ge(v_rest, 2 * s)
                    last = token_product("o", lambda i: o_hi[j][:, i, :], lambda i: o_lo[j][:, i, :],
                                         acc[j], half, True, True)
                    if half == 1:
                        last.then_inc(o_psum, 1)

                def step(s, n):
                    for k in range(H):
                        if has(n - 2):
                            scores_t(s - 2, n - 2, k)
                        if k < 2 and has(n - 3):
                            weighted(s - 3, n - 3, H - 2 + k)
                        if k >= 2 and has(n - 2):
                            weighted(s - 2, n - 2, k - 2)
                        now = list(scored(k)) if has(n - 1) else []
                        if k in (1, 3) and has(n):
                            transpose_x(s, n, k // 2)
                        if k in (5, 7) and has(n - 3):
                            transpose_o(s, n, (k - 5) // 2)
                        for u in now[:1]:
                            scores(s - 1, n - 1, u)
                        if k < 4 and has(n):
                            keys(s, n, k // 2, k % 2)
                        if 4 <= k < 8 and has(n - 1):
                            values(s, n, (k - 4) // 2, k % 2)
                        if 8 <= k < 12 and has(n):
                            queries(s, n, (k - 8) // 2, k % 2)
                        if k >= 12 and has(n - 3):
                            output(s, n, (k - 12) // 2, k % 2)
                        for u in now[1:]:
                            scores(s - 1, n - 1, u)
                        if k == 12 and has(n - 1):
                            maxima(s - 1, n - 1)

                pe.wait_ge(consts, 4)
                run(pe, step)


def channel_mix_pass(nc, psum, x1, g, wr_t, wk_t, wv_t, mu_r, mu_k, eye, out):
    B, S, D = x1.shape
    C = D // P
    TP = 2 * S
    T = TP // P
    STEPS = B // 2
    assert TP == BANK and C == 4 and T == 4

    with ExitStack() as weights_scope:
        def wsb(name, shape, dt):
            return weights_scope.enter_context(nc.sbuf_tensor(name, shape, dt))

        w_hi = {n: wsb(f"f{n}_hi", [P, C, D], F32R) for n in "rkv"}
        w_lo = {n: wsb(f"f{n}_lo", [P, C, D], F32R) for n in "rkv"}
        eye_sb = wsb("eye_f", [P, P], F32)
        mu = {n: wsb(f"mu_{n}_sb", [P, C], F32) for n in "rk"}
        one_minus_mu = {n: wsb(f"one_minus_mu_{n}", [P, C], F32) for n in "rk"}
        minus_half = wsb("minus_half_f", [P, T], F32)

        with ExitStack() as scope:
            def sem(name):
                return scope.enter_context(nc.semaphore(name))

            raw = {n: scope.enter_context(nc.sbuf_tensor(f"f{n}_raw", [P, C, D], F32)) for n in "rkv"}
            gate = scope.enter_context(nc.sbuf_tensor("gate_f", [P, 1], F32))
            w_in = {n: sem(f"f{n}_in") for n in "rkv"}
            small_in = sem("small_in_f")
            gate_ready = sem("gate_ready_f")
            gated = sem("gated_f")
            hi_ready = sem("w_hi_ready_f")
            lo_ready = sem("w_lo_ready_f")
            source = dict(r=wr_t, k=wk_t, v=wv_t)

            with nc.Block() as block:
                @block.sync
                def _(sp):
                    for dst, src in ((gate, g), (mu["r"], mu_r), (mu["k"], mu_k), (eye_sb, eye)):
                        sp.dma_start(dst[:, :], src).then_inc(small_in, DMA_INC)
                    for n in "kvr":
                        sp.dma_start(raw[n][:, :, :], source[n].rearrange("(c p) n -> p c n", p=P)).then_inc(w_in[n], DMA_INC)

                @block.scalar
                def _(act):
                    act.wait_ge(small_in, 4 * DMA_INC)
                    nc.scalar.activation(gate[:, :], gate[:, :], ACT.Tanh).then_inc(gate_ready, 1)
                    for n in "krv":
                        if n == "v":
                            act.wait_ge(gated, 1)
                        else:
                            act.wait_ge(w_in[n], DMA_INC)
                        nc.scalar.activation(w_hi[n][:, :, :], raw[n][:, :, :], ACT.Copy).then_inc(hi_ready, 1)

                @block.vector
                def _(dve):
                    nc.vector.memset(minus_half[:, :], -0.5).then_inc(lo_ready, 1)
                    dve.wait_ge(small_in, 4 * DMA_INC)
                    for n in "rk":
                        nc.vector.tensor_scalar(one_minus_mu[n][:, :], mu[n][:, :], -1.0, 1.0, ALU.mult, ALU.add)\
                            .then_inc(lo_ready, 1)
                    dve.wait_ge(gate_ready, 1)
                    dve.wait_ge(w_in["v"], DMA_INC)
                    nc.vector.tensor_scalar(raw["v"][:, :, :], raw["v"][:, :, :], gate[:, 0:1], 0.5,
                                            ALU.mult, ALU.mult).then_inc(gated, 1)
                    for i, n in enumerate("krv"):
                        dve.wait_ge(hi_ready, i + 1)
                        nc.vector.tensor_tensor(w_lo[n][:, :, :], raw[n][:, :, :], w_hi[n][:, :, :].bitcast(F32),
                                                ALU.subtract).then_inc(lo_ready, 1)
                    dve.wait_ge(lo_ready, 6)

        with ExitStack() as scope:
            def sb(name, shape, dt):
                return scope.enter_context(nc.sbuf_tensor(name, shape, dt))

            def sem(name):
                return scope.enter_context(nc.semaphore(name))

            x_sb = [[sb(f"y{i}_sb{j}", [P, D], F32) for j in range(T)] for i in range(2)]
            stats = sb("stats_f", [P, T, 6], F32)
            mean_var = sb("mean_var_f", [P, T, 2], F32)
            var_eps = sb("var_eps_f", [P, T], F32)
            rstd = sb("rstd_f", [P, T], F32)
            xn = sb("xn_f", [P, T, D], F32)
            xt = sb("xt_f", [P, C, 2, S + 1], F32)
            mixed = {n: sb(f"mixed_{n}", [P, C, TP], F32) for n in "rk"}
            m_hi = {n: sb(f"m{n}_hi", [P, C, TP], F32R) for n in "rk"}
            m_lo = {n: sb(f"m{n}_lo", [P, C, TP], F32R) for n in "rk"}
            kact = sb("kact", [P, C, TP], F32)
            kact_hi = sb("kact_hi", [P, C, TP], F32R)
            kact_lo = sb("kact_lo", [P, C, TP], F32R)
            tanh_r = sb("tanh_r", [P, T, D], F32)

            kv_bank = psum[0:4]
            r_bank = psum[4:6]
            t_bank = psum[6:8]

            zeroed = sem("zeroed")
            x_in = [[sem(f"y{i}_in{j}") for j in range(T)] for i in range(2)]
            ln_step = sem("ln_step_f")
            rstd_ready = sem("rstd_ready_f")
            xn_ready = sem("xn_ready_f")
            xt_psum = sem("xt_psum_f")
            xt_ready = sem("xt_ready_f")
            k_mixed = sem("k_mixed")
            k_hi = sem("k_hi_f")
            k_lo = sem("k_lo_f")
            r_mixed = sem("r_mixed")
            r_hi = sem("r_hi_f")
            r_lo = sem("r_lo_f")
            k_psum = sem("k_psum_f")
            relu_ready = sem("relu_ready")
            square_ready = sem("square_ready")
            act_hi = sem("act_hi")
            act_lo = sem("act_lo")
            r_psum = sem("r_psum")
            tanh_ready = sem("tanh_ready")
            v_psum = sem("v_psum_f")
            product_ready = sem("product_ready")
            out_ready = sem("out_ready")
            out_sent = [sem(f"out_sent{j}") for j in range(T)]

            FIRST_STEADY = 2
            LAST_STEADY = STEPS - 2
            assert (LAST_STEADY - FIRST_STEADY) % 2 == 0

            def run(eng, step):
                for s in range(-1, FIRST_STEADY):
                    step(s, s)
                with eng.Fori(0, (LAST_STEADY - FIRST_STEADY) // 2) as i:
                    for j in range(2):
                        step(2 * i + (FIRST_STEADY + j), FIRST_STEADY + j)
                for s in range(LAST_STEADY, STEPS):
                    step(s, s)

            def has(n):
                return 0 <= n < STEPS

            def rows(dram, s, j):
                return dram[2 * s + j // 2, (j % 2) * P:(j % 2 + 1) * P, :]

            block = scope.enter_context(nc.Block())

            @block.sync
            def _(sp):
                for j in range(T):
                    sp.dma_start(x_sb[0][j][:, :], rows(x1, 0, j)).then_inc(x_in[0][j], DMA_INC)

                def step(s, n):
                    for j in range(T):
                        if has(n):
                            sp.wait_ge(out_ready, T * s + j + 1)
                            sp.dma_start(rows(out, s, j), tanh_r[:, j, :]).then_inc(out_sent[j], DMA_INC)
                        if has(n + 2):
                            sp.dma_start(x_sb[n % 2][j][:, :], rows(x1, s + 2, j)).then_inc(x_in[n % 2][j], DMA_INC)

                run(sp, step)
                for j in range(T):
                    sp.wait_ge(out_sent[j], DMA_INC * STEPS)

            @block.gpsimd
            def _(pool):
                def step(s, n):
                    for c in range(C):
                        if has(n):
                            pool.wait_ge(relu_ready, C * s + c + 1)
                            nc.gpsimd.tensor_tensor(kact[:, c, :], kact[:, c, :], kact[:, c, :], ALU.mult)\
                                .then_inc(square_ready, 1)
                        if c == 0 and has(n + 1):
                            pool.wait_ge(ln_step, 9 * (s + 2))
                            nc.gpsimd.tensor_tensor(rstd[:, :], var_eps[:, :], minus_half[:, :], ALU.pow)\
                                .then_inc(rstd_ready, 1)
                    if has(n):
                        for j in range(T):
                            pool.wait_ge(product_ready, T * s + j + 1)
                            nc.gpsimd.tensor_tensor(tanh_r[:, j, :], tanh_r[:, j, :], x_sb[n % 2][j][:, :], ALU.add)\
                                .then_inc(out_ready, 1)

                run(pool, step)

            @block.scalar
            def _(act):
                def relu(s, n, c):
                    act.wait_ge(k_psum, C * s + c + 1)
                    if n > 0:
                        act.wait_ge(act_lo, C * s + c - C + 1)
                    nc.scalar.activation(kact[:, c, :], kv_bank[c][:, :], ACT.Relu).then_inc(relu_ready, 1)

                def square_hi(s, n, c):
                    act.wait_ge(square_ready, C * s + c + 1)
                    if n > 0:
                        act.wait_ge(v_psum, T * s)
                    nc.scalar.activation(kact_hi[:, c, :], kact[:, c, :], ACT.Copy).then_inc(act_hi, 1)

                def tanh(s, n, j):
                    act.wait_ge(r_psum, T * s + j + 1)
                    if n > 0:
                        act.wait_ge(out_sent[j], DMA_INC * s)
                    nc.scalar.activation(tanh_r[:, j, :], r_bank[j % 2][:, :], ACT.Tanh, scale=0.5)\
                        .then_inc(tanh_ready, 1)

                def transposed(s, n, c):
                    bank = t_bank[c % 2][:, :]
                    act.wait_ge(xt_psum, C * s + c + 1)
                    if n > 0:
                        act.wait_ge(r_lo, C * s - C + c + 1)
                    nc.scalar.activation(xt[:, c, :, 1:S + 1], bank.rearrange("p (b t) -> p b t", b=2), ACT.Copy)
                    nc.scalar.activation(mixed["k"][:, c, :], bank, ACT.Copy, scale=mu["k"][:, c:c + 1])
                    nc.scalar.activation(mixed["r"][:, c, :], bank, ACT.Copy, scale=mu["r"][:, c:c + 1])\
                        .then_inc(xt_ready, 1)

                def mixed_hi(s, n, c):
                    act.wait_ge(r_mixed, C * s + c + 1)
                    nc.scalar.activation(m_hi["r"][:, c, :], mixed["r"][:, c, :], ACT.Copy).then_inc(r_hi, 1)

                def step(s, n):
                    if has(n):
                        for c in range(C):
                            relu(s, n, c)
                            if c >= 1:
                                square_hi(s, n, c - 1)
                    for c in range(C):
                        if has(n):
                            tanh(s, n, c)
                            if c == 0:
                                square_hi(s, n, C - 1)
                        if has(n + 1):
                            transposed(s + 1, n + 1, c)
                    if has(n + 1):
                        for c in range(C):
                            mixed_hi(s + 1, n + 1, c)

                run(act, step)

            @block.vector
            def _(dve):
                nc.vector.memset(xt[:, :, :, 0:1], 0.0).then_inc(zeroed, 1)

                def statistics(s, n):
                    x = x_sb[n % 2]
                    if n > 0:
                        dve.wait_ge(ln_step, 9 * s)
                    for j in range(T):
                        dve.wait_ge(x_in[n % 2][j], DMA_INC // 2 * (s + (2 - n % 2)))
                        nc.vector.bn_stats(stats[:, j, :], x[j][:, :]).then_inc(ln_step, 1)

                def variance(s):
                    for j in range(T):
                        nc.vector.bn_aggr(mean_var[:, j, :], stats[:, j, :]).then_inc(ln_step, 1)
                    dve.wait_ge(ln_step, 9 * s + 2 * T)
                    nc.vector.tensor_scalar(var_eps[:, :], mean_var[:, :, 1], EPS, None, ALU.add).then_inc(ln_step, 1)

                def normalise(s, n):
                    dve.wait_ge(rstd_ready, s + 1)
                    if n > 0:
                        dve.wait_ge(xt_psum, C * s)
                    for j in range(T):
                        nc.vector.tensor_scalar(xn[:, j, :], x_sb[n % 2][j][:, :], mean_var[:, j, 0:1],
                                                rstd[:, j:j + 1], ALU.subtract, ALU.mult).then_inc(xn_ready, 1)

                def square_lo(s, c):
                    dve.wait_ge(act_hi, C * s + c + 1)
                    nc.vector.tensor_tensor(kact_lo[:, c, :], kact[:, c, :], kact_hi[:, c, :].bitcast(F32),
                                            ALU.subtract).then_inc(act_lo, 1)

                def mix(s, name, c, done):
                    m = mixed[name][:, c, :].rearrange("p (b t) -> p b t", b=2)
                    nc.vector.scalar_tensor_tensor(out=m, in0=xt[:, c, :, 0:S], scalar=one_minus_mu[name][:, c:c + 1],
                                                   in1=m, op0=ALU.mult, op1=ALU.add).then_inc(done, 1)

                def mix_k(s, n, c):
                    dve.wait_ge(xt_ready, C * s + c + 1)
                    mix(s, "k", c, k_mixed)
                    mix(s, "r", c, r_mixed)
                    if n > 0 and c == 0:
                        dve.wait_ge(k_psum, C * s)
                    dve.wait_ge(k_mixed, C * s + c + 1)
                    nc.vector.tensor_copy(m_hi["k"][:, c, :], mixed["k"][:, c, :]).then_inc(k_hi, 1)
                    dve.wait_ge(k_hi, C * s + c + 1)
                    nc.vector.tensor_tensor(m_lo["k"][:, c, :], mixed["k"][:, c, :], m_hi["k"][:, c, :].bitcast(F32),
                                            ALU.subtract).then_inc(k_lo, 1)

                def mix_r_lo(s, n, c):
                    dve.wait_ge(r_hi, C * s + c + 1)
                    nc.vector.tensor_tensor(m_lo["r"][:, c, :], mixed["r"][:, c, :], m_hi["r"][:, c, :].bitcast(F32),
                                            ALU.subtract).then_inc(r_lo, 1)

                def product(s, j):
                    dve.wait_ge(tanh_ready, T * s + j + 1)
                    dve.wait_ge(v_psum, T * s + j + 1)
                    nc.vector.scalar_tensor_tensor(out=tanh_r[:, j, :], in0=tanh_r[:, j, :], scalar=1.0,
                                                   in1=kv_bank[j][:, :], op0=ALU.add, op1=ALU.mult)\
                        .then_inc(product_ready, 1)

                def step(s, n):
                    if has(n + 1):
                        statistics(s + 1, n + 1)
                        dve.wait_ge(ln_step, 9 * (s + 1) + T)
                        if n >= 0:
                            dve.wait_ge(xn_ready, T * (s + 1))
                    if has(n):
                        square_lo(s, 0)
                    if has(n + 1):
                        variance(s + 1)
                    if has(n):
                        square_lo(s, 1)
                    if has(n + 1):
                        normalise(s + 1, n + 1)
                    if has(n):
                        for c in range(2, C):
                            square_lo(s, c)
                    if has(n + 1):
                        for c in range(C):
                            mix_k(s + 1, n + 1, c)
                    for c in range(C):
                        if has(n + 1):
                            mix_r_lo(s + 1, n + 1, c)
                        if has(n):
                            product(s, c)

                run(dve, step)

            @block.tensor
            def _(pe):
                def keys(s, n, c):
                    if c == 0:
                        pe.wait_ge(k_lo, C * (s + 1))
                    if n > 0:
                        pe.wait_ge(product_ready, T * s - T + c + 1)
                    cols = slice(c * P, (c + 1) * P)
                    for i in range(C):
                        nc.tensor.matmul(kv_bank[c][:, :], w_hi["k"][:, i, cols], m_hi["k"][:, i, :],
                                         start=(i == 0), stop=False)
                        nc.tensor.matmul(kv_bank[c][:, :], w_hi["k"][:, i, cols], m_lo["k"][:, i, :],
                                         start=False, stop=False)
                        last = nc.tensor.matmul(kv_bank[c][:, :], w_lo["k"][:, i, cols], m_hi["k"][:, i, :],
                                                start=False, stop=(i == C - 1))
                    last.then_inc(k_psum, 1)

                def token_product(w, hi, lo, bank, j):
                    at = slice(j * P, (j + 1) * P)
                    for i in range(C):
                        nc.tensor.matmul(bank[:, :], hi[:, i, at], w_hi[w][:, i, :], start=(i == 0), stop=False)
                        nc.tensor.matmul(bank[:, :], hi[:, i, at], w_lo[w][:, i, :], start=False, stop=False)
                        last = nc.tensor.matmul(bank[:, :], lo[:, i, at], w_hi[w][:, i, :], start=False,
                                                stop=(i == C - 1))
                    return last

                def receptance(s, n, j):
                    if j == 0:
                        pe.wait_ge(r_lo, C * (s + 1))
                    if n > 0 or j >= 2:
                        pe.wait_ge(tanh_ready, T * s + j - 1)
                    token_product("r", m_hi["r"], m_lo["r"], r_bank[j % 2], j).then_inc(r_psum, 1)

                def values(s, n, j):
                    if j == 0:
                        pe.wait_ge(act_lo, C * (s + 1))
                    pe.wait_ge(relu_ready, C * s + j + 1)
                    token_product("v", kact_hi, kact_lo, kv_bank[j], j).then_inc(v_psum, 1)

                def transposes(s, n, c):
                    if c == 0:
                        pe.wait_ge(xn_ready, T * (s + 1))
                    if n > 0 or c >= 2:
                        pe.wait_ge(xt_ready, C * s + c - 1)
                    for j in range(T):
                        last = nc.tensor.transpose(t_bank[c % 2][:, j * P:(j + 1) * P], xn[:, j, c * P:(c + 1) * P],
                                                   eye_sb[:, :])
                    last.then_inc(xt_psum, 1)

                def step(s, n):
                    if has(n):
                        for c in range(C):
                            keys(s, n, c)
                    for j in range(C):
                        if has(n):
                            receptance(s, n, j)
                        if has(n + 1):
                            transposes(s + 1, n + 1, j)
                    if has(n):
                        for j in range(T):
                            values(s, n, j)

                run(pe, step)


def build(nc, x, ctx_t, g_a, wq_t, bq, wk_t, bk, wv_t, bv, wo_t, bo, g_f, fr_t, fk_t, fv_t, mu_r, mu_k, eye,
          parts_dram, x1, out):
    with ExitStack() as scope:
        psum = [scope.enter_context(nc.psum_tensor(f"bank{i}", [P, BANK], F32)) for i in range(8)]
        attention_pass(nc, psum, x, ctx_t, g_a, wq_t, bq, wk_t, bk, wv_t, bv, wo_t, bo, eye, parts_dram, x1)
        channel_mix_pass(nc, psum, x1, g_f, fr_t, fk_t, fv_t, mu_r, mu_k, eye, out)


def kernel(**inputs):
    import numpy as _np
    import concourse.bacc as _bacc
    from concourse import mybir as _mybir
    from concourse.bass_utils import run_bass_kernel_spmd as _run

    a = {n: _np.asarray(v) for n, v in inputs.items()}
    B, S, D = a["x"].shape

    def t(w):
        return _np.ascontiguousarray(w.T)

    def column(v):
        return _np.ascontiguousarray(v.reshape(D // P, P).T)

    def everywhere(v):
        return _np.ascontiguousarray(_np.broadcast_to(v.reshape(1, 1), (P, 1)))

    data = dict(
        x=a["x"], ctx_t=_np.ascontiguousarray(a["ctx_1024"].transpose(0, 2, 1)), g_a=everywhere(a["g_xattn"]),
        wq_t=t(a["L0_xattn_Wq"]), bq=column(a["L0_xattn_bq"]), wk_t=t(a["L0_xattn_Wk"]), bk=column(a["L0_xattn_bk"]),
        wv_t=t(a["L0_xattn_Wv"]), bv=column(a["L0_xattn_bv"]), wo_t=t(a["L0_xattn_Wo"]),
        bo=_np.ascontiguousarray(a["L0_xattn_bo"].reshape(1, D)), g_f=everywhere(a["g_ffn"]),
        fr_t=t(a["L0_ffn_W_r"]), fk_t=t(a["L0_ffn_W_k"]), fv_t=t(a["L0_ffn_W_v"]),
        mu_r=column(a["L0_ffn_mu_r"]), mu_k=column(a["L0_ffn_mu_k"]), eye=_np.eye(P, dtype=_np.float32),
    )
    nc = _bacc.Bacc("TRN2", target_bir_lowering=False, num_devices=1)
    arrays, args = {}, {}
    for name, v in data.items():
        v = _np.ascontiguousarray(v)
        arrays[f"in_{name}"] = v
        args[name] = nc.dram_tensor(f"in_{name}", v.shape, _mybir.dt.from_np(v.dtype), kind="ExternalInput").ap()
    args["x1"] = nc.dram_tensor("x1_dram", (B, S, D), F32, kind="Internal").ap()
    args["parts_dram"] = nc.dram_tensor("parts_dram", (2, 2, D, 2, S), F32, kind="Internal").ap()
    args["out"] = nc.dram_tensor("out_0", (B, S, D), F32, kind="ExternalOutput").ap()
    build(nc, **args)
    r = _run(nc, [arrays], core_ids=[0])
    return r.results[0]["out_0"]
```

```python
import math
from contextlib import ExitStack

import concourse.bass as bass
from concourse import mybir


P = 128
BANK = 512
EPS = 1e-5
DMA_INC = 16

ALU = mybir.AluOpType
ACT = mybir.ActivationFunctionType
AX = mybir.AxisListType
F32 = mybir.dt.float32
F32R = mybir.dt.float32r
F16 = mybir.dt.float16
BF16 = mybir.dt.bfloat16


def attention_pass(nc, psum, w_hi, w_lo, eye_sb, minus_half, mix_weights, x, ctx_t, g, wq_t, bq, wk_t, bk, wv_t, bv,
                   wo_t, bo, eye, parts_dram, x1):
    B, S, D = x.shape
    C = D // P
    HD = 32
    H = D // HD
    HC = P // HD
    T = S // P
    SCALE = float(HD) ** -0.5
    VPARTS = 3
    VW = VPARTS * HD + 1
    KROWS = 3 * HD
    MROW = KROWS
    SROWS = KROWS + 2
    SHIFT = 12 * math.log(2.0) / SCALE
    PAIRS = C // 2
    HP = H // PAIRS
    STACK = DMA_INC * 3
    HG = 2
    G = H // HG
    assert S == 2 * P and T == 2 and D == BANK and C == 4

    with ExitStack() as scope:
        def sb(name, shape, dt):
            return scope.enter_context(nc.sbuf_tensor(name, shape, dt))

        def sem(name):
            return scope.enter_context(nc.semaphore(name))

        def over(names):
            with ExitStack() as early:
                return {n: early.enter_context(nc.sbuf_tensor(f"{n}_raw", [P, C, D], F32)) for n in names}

        raw = over("kqvo")
        k_stack_odd = sb("k_stack1", [P, H, S], F32R)
        q_stack_odd = sb("q_stack1", [P, H, S], F32R)
        mix_raw = over(("mix_k", "mix_r", "mix_v"))
        xn_hi = sb("xn_hi", [P, C, S], F32R)
        xn_lo = sb("xn_lo", [P, C, S], F32R)
        parts = sb("parts", [P, C, 2, S], F32R)
        ctx_hi = [sb(f"ctx_hi{i}", [P, C, S], F32R) for i in range(2)]
        ctx_lo = [sb(f"ctx_lo{i}", [P, C, S], F32R) for i in range(2)]
        q_stack = [sb("q_stack0", [P, H, S], F32R), q_stack_odd]
        k_stack = [sb("k_stack0", [P, H, S], F32R), k_stack_odd]
        bq_sb = sb("bq_sb", [P, C], F32)
        bk_sb = sb("bk_sb", [P, C], F32)
        bv_sb = sb("bv_sb", [P, C], F32)
        gate = sb("gate_a", [P, 1], F32)
        out_bias = sb("out_bias", [P, D], F32)
        x_sb = [sb(f"x_sb{j}", [P, D], F32) for j in range(T)]
        stats = sb("stats_a", [P, T, 6], F32)
        mean_var = sb("mean_var_a", [P, T, 2], F32)
        var_eps = sb("var_eps_a", [P, T], F32)
        rstd = sb("rstd_a", [P, T], F32)
        ctx_raw = sb("ctx_raw", [P, C, S], F32)
        v_sb = [sb(f"v_sb{i}", [P, T, H, VW], BF16) for i in range(2)]
        row_max = sb("row_max", [P, H, T], F32)
        max_row = sb("max_row", [H * T, 2, P], F32R)
        probs = sb("probs", [P, T, S], F32)
        probs_hi = [sb(f"probs_hi{i}", [P, T, S], F16) for i in range(2)]
        probs_lo = [sb(f"probs_lo{i}", [P, T, S], F16) for i in range(2)]
        inv_sum = sb("inv_sum", [P, HG, T], F32)
        o_sum = sb("o_sum", [P, HG, T, HD], F32)
        o_first = [sb(f"o_first{i}", [P, T, HC, HD], F32) for i in range(2)]
        o_rest = [sb(f"o_rest{c}", [P, T, HC, HD], F32) for c in range(1, C)]
        o_hi = [sb(f"o_hi{j}", [P, C, P], F32R) for j in range(T)]
        o_lo = [sb(f"o_lo{j}", [P, C, P], F32R) for j in range(T)]
        res = [sb(f"res{j}", [P, D], F32) for j in range(T)]

        ones_row = o_rest[0][0:1, 0, :, :].rearrange("p h d -> p (h d)")

        acc = psum[0:2]
        s_bank = psum[2:4]
        st_bank = psum[4:6]
        pv_bank = psum[6:8]

        consts = sem("consts")
        minus_rows = sem("minus_rows")
        biases_in = sem("biases_in")
        output_small_in = sem("output_small_in")
        w_in = {n: sem(f"w{n}_in") for n in "qkvo"}
        w_hi_ready = {n: sem(f"w{n}_hi_ready") for n in "qkvo"}
        w_lo_ready = {n: sem(f"w{n}_lo_ready") for n in "qkvo"}
        gate_ready = sem("gate_ready_a")
        gated = sem("gated_a")
        bias_psum = sem("bias_psum")
        bias_ready = sem("bias_ready")
        mix_in = {n: sem(f"f{n}_in") for n in "rkv"}
        mix_small_in = sem("mix_small_in")
        mix_hi_ready = {n: sem(f"f{n}_hi_ready") for n in "rkv"}
        mix_ready = sem("mix_ready")
        mix_gate_ready = sem("mix_gate_ready")
        mix_gated = sem("mix_gated")
        x_in = [sem(f"x_in{j}") for j in range(T)]
        ln_step = sem("ln_step")
        rstd_ready = sem("rstd_ready")
        xn_ready = sem("xn_ready")
        xt_psum = sem("xt_psum")
        xt_hi = sem("xt_hi")
        xt_lo = sem("xt_lo")
        ctx_in = sem("ctx_in")
        ctx_hi_ready = sem("ctx_hi_ready")
        ctx_lo_ready = sem("ctx_lo_ready")
        k_psum = sem("k_psum")
        k_hi_ready = sem("k_hi_ready")
        k_lo_ready = sem("k_lo_ready")
        q_psum = sem("q_psum")
        q_hi_ready = sem("q_hi_ready")
        q_lo_ready = sem("q_lo_ready")
        k_saved = [sem(f"k_saved{i}") for i in range(PAIRS)]
        q_saved = [sem(f"q_saved{i}") for i in range(PAIRS)]
        k_stacked = [sem(f"k_stacked{i}") for i in range(PAIRS)]
        q_stacked = [sem(f"q_stacked{i}") for i in range(PAIRS)]
        v_psum = sem("v_psum")
        v1_ready = sem("v1_ready")
        v_rest = sem("v_rest")
        v2_ready = sem("v2_ready")
        v_ready = sem("v_ready")
        s_psum = sem("s_psum")
        max_ready = sem("max_ready")
        max_psum = sem("max_psum")
        max_copied = sem("max_copied")
        max_stacked = sem("max_stacked")
        st_psum = sem("st_psum")
        probs_ready = sem("probs_ready")
        probs_lo_ready = sem("probs_lo_ready")
        pv_psum = sem("pv_psum")
        pv_read = sem("pv_read")
        o_ready = sem("o_ready")
        ot_psum = sem("ot_psum")
        ot_hi = sem("ot_hi")
        ot_lo = sem("ot_lo")
        o_psum = sem("o_psum")
        res_in = [sem(f"res_in{j}") for j in range(T)]
        res_biased = sem("res_biased")
        x1_ready = sem("x1_ready")
        x1_out = [sem(f"x1_out{j}") for j in range(T)]

        SCORE_SLOTS = (0, 1, 2, 2, 1, 2, 1, 2, 1, 2, 1, 1)
        FIRST_SCORE_SLOTS = (0, 0, 0, 0, 2, 2, 2, 2, 2, 2, 2, 2)
        assert sum(SCORE_SLOTS) == H and sum(FIRST_SCORE_SLOTS) == H
        FIRST_STEADY = 4
        LAST_STEADY = B - 2
        assert (LAST_STEADY - FIRST_STEADY) % 2 == 0

        def run(eng, step):
            for s in range(-1, FIRST_STEADY):
                step(s, s)
            with eng.Fori(0, (LAST_STEADY - FIRST_STEADY) // 2) as i:
                for j in range(2):
                    step(2 * i + (FIRST_STEADY + j), FIRST_STEADY + j)
            for s in range(LAST_STEADY, B + 4):
                step(s, s)

        def has(n):
            return 0 <= n < B

        def chunks(w):
            return w.rearrange("(c p) n -> p c n", p=P)

        def split_hi(n, raw, done):
            nc.scalar.activation(w_hi[n][:, :, :], raw[:, :, :], ACT.Copy).then_inc(done, 1)

        def split_lo(n, raw, done):
            nc.vector.tensor_tensor(w_lo[n][:, :, :], raw[:, :, :], w_hi[n][:, :, :].bitcast(F32),
                                    ALU.subtract).then_inc(done, 1)

        def scored(n, k):
            slots = FIRST_SCORE_SLOTS if n == 1 else SCORE_SLOTS
            return range(sum(slots[:k]), sum(slots[:k + 1])) if has(n - 1) and k < len(slots) else range(0)

        def o_chunk(n, c):
            return o_first[n % 2] if c == 0 else o_rest[c - 1]

        block = scope.enter_context(nc.Block())

        @block.sync
        def _(sp):
            def save(b, n, pair, which, ready, saved):
                sp.wait_ge(ready, 2 * b + pair + 1)
                cs = slice(2 * pair, 2 * pair + 2)
                dst = parts_dram[which, n % 2, :, :, :].rearrange("(c p) a t -> p c (a t)", p=P)
                sp.dma_start(dst[:, cs, :], parts[:, cs, :, :].rearrange("p c a t -> p c (a t)").bitcast(F32)).then_inc(saved[pair], DMA_INC)

            def stack(b, n, pair, which, dst, order, saved, stacked):
                if n == 1 and pair == 0:
                    sp.wait_ge(w_lo_ready["qo"[which]], 1)
                sp.wait_ge(saved[pair], DMA_INC * (b + 1))
                hs = slice(HP * pair, HP * pair + HP)
                for i, part in enumerate(order):
                    src = parts_dram[which, n % 2, :, part, :].rearrange("(h p) t -> p h t", p=HD)
                    sp.dma_start(dst[n % 2][HD * i:HD * i + HD, hs, :].bitcast(F32), src[:, hs, :])\
                        .then_inc(stacked[pair], DMA_INC)

            def stack_k(b, n, pair, through):
                if n >= 2 and not through:
                    sp.wait_ge(st_psum, H * (b - 2) + (pair + 1) * HP)
                stack(b, n, pair, 0, k_stack, (0, 1, 0), k_saved, k_stacked)

            def stack_q(b, n, pair):
                stack(b, n, pair, 1, q_stack, (0, 0, 1), q_saved, q_stacked)

            def stack_maxima(b, n):
                sp.wait_ge(max_copied, 2 * (b + 1))
                for i in range(2):
                    row = q_stack[n % 2][MROW + i:MROW + i + 1, :, :].rearrange("o h (j t) -> o (h j) t", j=T)
                    sp.dma_start(row.bitcast(F32), max_row[:, i, :].bitcast(F32)).then_inc(max_stacked, DMA_INC)

            def store(b, j):
                sp.wait_ge(x1_ready, 2 * b + j + 1)
                sp.dma_start(x1[b, j * P:(j + 1) * P, :], res[j][:, :]).then_inc(x1_out[j], DMA_INC)

            def step(s, n):
                if has(n - 4):
                    store(s - 4, 1)
                if has(n - 1):
                    stack_k(s - 1, n - 1, 1, has(n - 4))
                    stack_q(s - 1, n - 1, 1)
                if has(n + 1):
                    for j in range(T):
                        if n >= 0:
                            sp.wait_ge(xt_psum, 2 * s + j + 1)
                        sp.dma_start(x_sb[j][:, :], x[s + 1, j * P:(j + 1) * P, :]).then_inc(x_in[j], DMA_INC)
                    if n >= 0:
                        sp.wait_ge(ctx_lo_ready, 2 * (s + 1))
                    sp.dma_start(ctx_raw[:, :, :], ctx_t[s + 1, :, :].rearrange("(c p) t -> p c t", p=P))\
                        .then_inc(ctx_in, DMA_INC)
                if has(n):
                    save(s, n, 0, 0, k_lo_ready, k_saved)
                    save(s, n, 1, 0, k_lo_ready, k_saved)
                if has(n - 3):
                    for j in range(T):
                        if has(n - 1):
                            sp.wait_ge(v_ready, 2 * (s - 1) + j + 1)
                        elif n >= 4:
                            sp.wait_ge(x1_out[j], DMA_INC * (s - 3))
                        sp.dma_start(res[j][:, :], x[s - 3, j * P:(j + 1) * P, :]).then_inc(res_in[j], DMA_INC)
                if has(n):
                    stack_k(s, n, 0, has(n - 3) and has(n - 1))
                    save(s, n, 0, 1, q_lo_ready, q_saved)
                if has(n - 1):
                    stack_maxima(s - 1, n - 1)
                if has(n):
                    stack_q(s, n, 0)
                    save(s, n, 1, 1, q_lo_ready, q_saved)
                if has(n - 3):
                    store(s - 3, 0)
                if n == -1:
                    load_weights()
                if n == B:
                    load_mix_weights()

            def load_weights():
                for dst, src in ((eye_sb, eye), (bq_sb, bq), (bk_sb, bk)):
                    sp.dma_start(dst[:, :], src).then_inc(biases_in, DMA_INC)
                for n, w in (("k", wk_t), ("q", wq_t), ("v", wv_t), ("o", wo_t)):
                    sp.dma_start(raw[n][:, :, :], chunks(w)).then_inc(w_in[n], DMA_INC)
                for dst, src in ((gate[:, :], g), (bv_sb[:, :], bv), (out_bias[0:1, :], bo)):
                    sp.dma_start(dst, src).then_inc(output_small_in, DMA_INC)

            def load_mix_weights():
                for dst, src in mix_weights["small"]:
                    sp.dma_start(dst[:, :], src).then_inc(mix_small_in, DMA_INC)
                sp.wait_ge(q_psum, 2 * B)
                sp.dma_start(mix_raw["mix_k"][:, :, :], chunks(mix_weights["k"])).then_inc(mix_in["k"], DMA_INC)
                for pair in range(PAIRS):
                    sp.wait_ge(q_saved[pair], DMA_INC * B)
                sp.dma_start(mix_raw["mix_r"][:, :, :], chunks(mix_weights["r"])).then_inc(mix_in["r"], DMA_INC)
                sp.wait_ge(v_psum, 2 * B)
                sp.dma_start(mix_raw["mix_v"][:, :, :], chunks(mix_weights["v"])).then_inc(mix_in["v"], DMA_INC)

            run(sp, step)
            for j in range(T):
                sp.wait_ge(x1_out[j], DMA_INC * B)

        @block.gpsimd
        def _(pool):
            def probs_rest(b, n, u):
                pool.wait_ge(probs_ready, H * b + u + 1)
                nc.gpsimd.tensor_tensor(probs_lo[u % 2][:, :, :], probs[:, :, :], probs_hi[u % 2][:, :, :],
                                        ALU.subtract).then_inc(probs_lo_ready, 1)

            def context_lo(b, n, half):
                pool.wait_ge(ctx_hi_ready, 2 * b + half + 1)
                cs = slice(half * C // 2, (half + 1) * C // 2)
                nc.gpsimd.tensor_tensor(ctx_lo[n % 2][:, cs, :], ctx_raw[:, cs, :],
                                        ctx_hi[n % 2][:, cs, :].bitcast(F32), ALU.subtract).then_inc(ctx_lo_ready, 1)

            def bias(b, n, j):
                if n == 0 and j == 0:
                    pool.wait_ge(bias_ready, 2)
                pool.wait_ge(res_in[j], DMA_INC * (b + 1))
                nc.gpsimd.tensor_tensor(res[j][:, :], res[j][:, :], out_bias[:, :], ALU.add).then_inc(res_biased, 1)

            def step(s, n):
                if n == 0:
                    pool.wait_ge(w_lo_ready["k"], 1)
                    pool.wait_ge(w_lo_ready["q"], 1)
                    for i, stack in enumerate(k_stack):
                        nc.gpsimd.memset(stack[MROW:SROWS, :, :].bitcast(F32), -1.0).then_inc(minus_rows, 1)
                        pool.wait_ge(minus_rows, i + 1)
                for k in range(H):
                    if k in (9, 12) and has(n + 1):
                        context_lo(s + 1, n + 1, (k - 9) // 3)
                    if k in (10, 14) and has(n - 3):
                        bias(s - 3, n - 3, (k - 10) // 4)
                    if k == 13 and has(n + 1):
                        if n == -1:
                            pool.wait_ge(consts, 1)
                        pool.wait_ge(ln_step, 5 * (s + 2))
                        nc.gpsimd.tensor_tensor(rstd[:, :], var_eps[:, :], minus_half[:, 0:T], ALU.pow)\
                            .then_inc(rstd_ready, 1)
                    if has(n - 2) and n <= B:
                        probs_rest(s - 2, n - 2, k)

            run(pool, step)

        @block.scalar
        def _(act):
            def exp_hi(b, n, u):
                act.wait_ge(st_psum, H * b + u + 1)
                if n > 0 or u >= 2:
                    act.wait_ge(pv_psum, H * b + u - 1)
                nc.scalar.activation(probs_hi[u % 2][:, :, :].rearrange("p a t -> p (a t)"), st_bank[u % 2][:, :],
                                     ACT.Exp, scale=SCALE)

            def exp(b, n, u):
                if n > 0 or u > 0:
                    act.wait_ge(probs_lo_ready, H * b + u)
                nc.scalar.activation(probs[:, :, :].rearrange("p a t -> p (a t)"), st_bank[u % 2][:, :],
                                     ACT.Exp, scale=SCALE).then_inc(probs_ready, 1)

            def transposed_hi(b, n, j):
                act.wait_ge(xt_psum, 2 * b + j + 1)
                if n > 0:
                    act.wait_ge(q_psum, 2 * b)
                nc.scalar.activation(xn_hi[:, :, j * P:(j + 1) * P], acc[1 - j][:, :].rearrange("p (c t) -> p c t", c=C),
                                     ACT.Copy).then_inc(xt_hi, 1)

            def projected_hi(b, n, pair, bias, bank, done, ready):
                act.wait_ge(done, 2 * b + pair + 1)
                if n == 0:
                    act.wait_ge(biases_in, 3 * DMA_INC)
                if done is q_psum:
                    act.wait_ge(k_saved[pair], DMA_INC * (b + 1))
                elif n > 0:
                    act.wait_ge(q_saved[pair], DMA_INC * b)
                for c in range(2 * pair, 2 * pair + 2):
                    at = (c % 2) * S
                    last = nc.scalar.activation(parts[:, c, 0, :], bank[:, at:at + S], ACT.Identity, bias=bias[:, c:c + 1])
                last.then_inc(ready, 1)

            def value_part(n, j, i):
                return v_sb[n % 2][:, j, :, i * HD:(i + 1) * HD]

            def values_1(b, n, j):
                act.wait_ge(v_psum, 2 * b + j + 1)
                if n >= 2:
                    act.wait_ge(pv_psum, H * (b - 1))
                nc.scalar.activation(value_part(n, j, 0), acc[j][:, :].rearrange("p (h d) -> p h d", h=H),
                                     ACT.Copy).then_inc(v1_ready, 1)

            def values_2(b, n, j):
                act.wait_ge(v_rest, 2 * b + j + 1)
                nc.scalar.activation(value_part(n, j, 1), res[j][:, :].rearrange("p (h d) -> p h d", h=H),
                                     ACT.Copy).then_inc(v2_ready, 1)

            def output_hi(b, n, j):
                act.wait_ge(ot_psum, 2 * b + j + 1)
                if n > 0:
                    act.wait_ge(o_psum, 2 * b + j - 1)
                nc.scalar.activation(o_hi[j][:, :, :], acc[1 - j][:, :].rearrange("p (c t) -> p c t", c=C),
                                     ACT.Copy).then_inc(ot_hi, 1)

            def step(s, n):
                for k in range(H):
                    if k in (2, 4) and has(n):
                        projected_hi(s, n, k // 2 - 1, bk_sb, acc[k // 2 - 1], k_psum, k_hi_ready)
                    if k in (6, 8) and has(n - 1):
                        values_1(s - 1, n - 1, (k - 6) // 2)
                    if k in (10, 12) and has(n):
                        i = (k - 10) // 2
                        projected_hi(s, n, i, bq_sb, acc[i], q_psum, q_hi_ready)
                    if has(n - 2):
                        exp_hi(s - 2, n - 2, k)
                    if k in (1, 3) and has(n):
                        transposed_hi(s, n, k // 2)
                    if k in (5, 7) and has(n - 3):
                        output_hi(s - 3, n - 3, (k - 5) // 2)
                    if k in (7, 9) and has(n - 1):
                        values_2(s - 1, n - 1, (k - 7) // 2)
                    if has(n - 2):
                        exp(s - 2, n - 2, k)
                    if (n, k) in ((-1, 14), (-1, 15), (0, 5)):
                        w = "kqv"[((-1, 14), (-1, 15), (0, 5)).index((n, k))]
                        act.wait_ge(w_in[w], DMA_INC)
                        split_hi(w, raw[w], w_hi_ready[w])
                    if n == 1 and k == 0:
                        act.wait_ge(output_small_in, 3 * DMA_INC)
                        nc.scalar.activation(gate[:, :], gate[:, :], ACT.Tanh).then_inc(gate_ready, 1)
                    if n == 1 and k == 2:
                        act.wait_ge(gated, 1)
                        split_hi("o", raw["o"], w_hi_ready["o"])
                    if n == B and k == 15:
                        act.wait_ge(mix_small_in, 3 * DMA_INC)
                        mix_gate = mix_weights["gate"]
                        nc.scalar.activation(mix_gate[:, :], mix_gate[:, :], ACT.Tanh).then_inc(mix_gate_ready, 1)
                    if n == B + 2 and k in (8, 9):
                        w, at = (("k", "k"), ("r", "q"))[k - 8]
                        act.wait_ge(mix_in[w], DMA_INC)
                        split_hi(at, mix_raw["mix_" + w], mix_hi_ready[w])
                    if n == B + 2 and k == 10:
                        act.wait_ge(mix_gated, 1)
                        split_hi("v", mix_raw["mix_v"], mix_hi_ready["v"])
                    if k in (8, 11) and has(n + 1):
                        cs = slice(0, C // 2) if k == 8 else slice(C // 2, C)
                        act.wait_ge(ctx_in, DMA_INC * (s + 2))
                        if n >= 1 and k == 8:
                            act.wait_ge(v_psum, 2 * s)
                        nc.scalar.activation(ctx_hi[(n + 1) % 2][:, cs, :], ctx_raw[:, cs, :], ACT.Copy)\
                            .then_inc(ctx_hi_ready, 1)
            run(act, step)

        @block.vector
        def _(dve):
            nc.vector.memset(minus_half[:, :], -0.5).then_inc(consts, 1)
            nc.vector.memset(ones_row, 1.0).then_inc(consts, 1)
            for i in range(2):
                nc.vector.memset(v_sb[i][:, :, :, VW - 1:VW], 1.0).then_inc(consts, 1)

            def probs_rest(b, n, u):
                dve.wait_ge(probs_ready, H * b + u + 1)
                nc.vector.tensor_tensor(probs_lo[u % 2][:, :, :], probs[:, :, :], probs_hi[u % 2][:, :, :],
                                        ALU.subtract).then_inc(probs_lo_ready, 1)

            def output_weights(k):
                if k == 0:
                    dve.wait_ge(gate_ready, 1)
                    dve.wait_ge(w_in["o"], DMA_INC)
                    wo = raw["o"][:, :, :]
                    nc.vector.tensor_scalar(wo, wo, gate[:, 0:1], None, ALU.mult).then_inc(gated, 1)
                if k == 4:
                    dve.wait_ge(bias_psum, 1)
                    nc.vector.scalar_tensor_tensor(out=out_bias[0:1, :], in0=out_bias[0:1, :], scalar=gate[0:1, 0:1],
                                                   in1=pv_bank[0][0:1, :], op0=ALU.mult, op1=ALU.add).then_inc(bias_ready, 1)
                    dve.wait_ge(w_hi_ready["o"], 1)
                    split_lo("o", raw["o"], w_lo_ready["o"])
                if k == 8:
                    dve.wait_ge(bias_psum, 2)
                    nc.vector.tensor_copy(out_bias[:, :], pv_bank[1][:, :]).then_inc(bias_ready, 1)

            def mix_weights_ready(n, k):
                if (n, k) == (B + 1, 0):
                    dve.wait_ge(mix_small_in, 3 * DMA_INC)
                    for mu, one_minus_mu in mix_weights["mu"]:
                        nc.vector.tensor_scalar(one_minus_mu[:, :], mu[:, :], -1.0, 1.0, ALU.mult, ALU.add)\
                            .then_inc(mix_ready, 1)
                if (n, k) == (B + 2, 6):
                    dve.wait_ge(mix_gate_ready, 1)
                    dve.wait_ge(mix_in["v"], DMA_INC)
                    wv = mix_raw["mix_v"][:, :, :]
                    nc.vector.tensor_scalar(wv, wv, mix_weights["gate"][:, 0:1], 0.5, ALU.mult, ALU.mult)\
                        .then_inc(mix_gated, 1)
                if n == B + 2 and k in (8, 9, 15):
                    w, at = {8: ("k", "k"), 9: ("r", "q"), 15: ("v", "v")}[k]
                    dve.wait_ge(mix_hi_ready[w], 1)
                    split_lo(at, mix_raw["mix_" + w], mix_ready)

            def residual(b, j):
                dve.wait_ge(o_psum, 2 * b + j + 1)
                dve.wait_ge(res_biased, 2 * b + j + 1)
                nc.vector.tensor_tensor(res[j][:, :], acc[j][:, :], res[j][:, :], ALU.add).then_inc(x1_ready, 1)

            def normalise(b, n, grp):
                bank = pv_bank[grp % 2][:, 0:HG * T * VW].rearrange("p (u v) -> p u v", v=VW)
                chunk, h = grp * HG // HC, grp * HG % HC
                out = o_chunk(n, chunk)[:, :, h:h + HG, :].rearrange("p j h d -> p h j d")
                dve.wait_ge(pv_psum, H * b + HG * (grp + 1))
                if n > 0 or grp > 0:
                    dve.wait_ge(o_ready, G * b + grp)
                nc.vector.reciprocal(inv_sum[:, :, :].rearrange("p h j -> p (h j)"), bank[:, :, VW - 1]).then_inc(pv_read, 1)
                nc.vector.tensor_reduce(o_sum[:, :, :, :].rearrange("p h j d -> p (h j) d"),
                                        bank[:, :, 0:VW - 1].rearrange("p u (i d) -> p u d i", i=VPARTS),
                                        AX.X, ALU.add).then_inc(pv_read, 1)
                if grp == 0 and n >= 2:
                    dve.wait_ge(ot_psum, 2 * (b - 1))
                elif h == 0 and chunk > 0 and n > 0:
                    dve.wait_ge(ot_psum, 2 * b)
                dve.wait_ge(pv_read, 2 * (G * b + grp + 1))
                nc.vector.tensor_tensor(out, o_sum[:, :, :, :],
                                        inv_sum[:, :, :].unsqueeze(3).to_broadcast([P, HG, T, HD]),
                                        ALU.mult).then_inc(o_ready, 1)

            def values_rest(b, n, j):
                dve.wait_ge(v1_ready, 2 * b + j + 1)
                if n > 0:
                    dve.wait_ge(v_ready, 2 * b + j - 1)
                if n >= 3:
                    dve.wait_ge(x1_out[j], DMA_INC * (b - 2))
                part = v_sb[n % 2][:, j, :, 0:HD]
                nc.vector.tensor_tensor(res[j][:, :].rearrange("p (h d) -> p h d", h=H),
                                        acc[j][:, :].rearrange("p (h d) -> p h d", h=H), part,
                                        ALU.subtract).then_inc(v_rest, 1)

            def values_3(b, n, j):
                dve.wait_ge(v2_ready, 2 * b + j + 1)
                v = v_sb[n % 2][:, j, :, :]
                nc.vector.tensor_tensor(v[:, :, 2 * HD:3 * HD], res[j][:, :].rearrange("p (h d) -> p h d", h=H),
                                        v[:, :, HD:2 * HD], ALU.subtract).then_inc(v_ready, 1)

            def transposed_lo(b, j):
                dve.wait_ge(xt_hi, 2 * b + j + 1)
                at = slice(j * P, (j + 1) * P)
                nc.vector.tensor_tensor(xn_lo[:, :, at], acc[1 - j][:, :].rearrange("p (c t) -> p c t", c=C),
                                        xn_hi[:, :, at].bitcast(F32), ALU.subtract).then_inc(xt_lo, 1)

            def projected_lo(b, pair, bias, bank, hi_ready, lo_ready):
                dve.wait_ge(hi_ready, 2 * b + pair + 1)
                for c in range(2 * pair, 2 * pair + 2):
                    at = (c % 2) * S
                    last = nc.vector.scalar_tensor_tensor(out=parts[:, c, 1, :], in0=bank[:, at:at + S],
                                                          scalar=bias[:, c:c + 1], in1=parts[:, c, 0, :].bitcast(F32),
                                                          op0=ALU.add, op1=ALU.subtract)
                last.then_inc(lo_ready, 1)

            def output_lo(b, j):
                dve.wait_ge(ot_hi, 2 * b + j + 1)
                nc.vector.tensor_tensor(o_lo[j][:, :, :], acc[1 - j][:, :].rearrange("p (c t) -> p c t", c=C),
                                        o_hi[j][:, :, :].bitcast(F32), ALU.subtract).then_inc(ot_lo, 1)

            def maximum(b, n, u):
                dve.wait_ge(s_psum, H * b + u + 1)
                if n > 0 and u == 0:
                    dve.wait_ge(max_psum, b)
                nc.vector.tensor_reduce(row_max[:, u, :], s_bank[u % 2][:, :].rearrange("p (j t) -> p j t", j=T),
                                        AX.X, ALU.max).then_inc(max_ready, 1)

            def statistics(b, n):
                if n > 0:
                    dve.wait_ge(ln_step, 5 * b)
                for j in range(T):
                    dve.wait_ge(x_in[j], DMA_INC * (b + 1))
                    nc.vector.bn_stats(stats[:, j, :], x_sb[j][:, :]).then_inc(ln_step, 1)

            def variance(b):
                for j in range(T):
                    nc.vector.bn_aggr(mean_var[:, j, :], stats[:, j, :]).then_inc(ln_step, 1)
                dve.wait_ge(ln_step, 5 * b + 2 * T)
                nc.vector.tensor_scalar(var_eps[:, :], mean_var[:, :, 1], EPS, None, ALU.add).then_inc(ln_step, 1)

            def layer_norm(b):
                dve.wait_ge(rstd_ready, b + 1)
                for j in range(T):
                    nc.vector.tensor_scalar(x_sb[j][:, :], x_sb[j][:, :], mean_var[:, j, 0:1], rstd[:, j:j + 1],
                                            ALU.subtract, ALU.mult).then_inc(xn_ready, 1)

            def step(s, n):
                for k in range(H):
                    if n == B + 1:
                        probs_rest(s - 2, n - 2, k)
                    if k == 0 and has(n - 4):
                        residual(s - 4, 1)
                    if k == 13 and has(n - 1):
                        dve.wait_ge(max_psum, s)
                        if n >= 2:
                            dve.wait_ge(max_stacked, 2 * DMA_INC * (s - 1))
                        nc.vector.tensor_scalar(max_row[:, 0, :], s_bank[0][0:H * T, 0:P], -SHIFT, None,
                                                ALU.add).then_inc(max_copied, 1)
                        dve.wait_ge(max_copied, 2 * s - 1)
                        nc.vector.scalar_tensor_tensor(out=max_row[:, 1, :], in0=s_bank[0][0:H * T, 0:P],
                                                       scalar=-SHIFT, in1=max_row[:, 0, :].bitcast(F32),
                                                       op0=ALU.add, op1=ALU.subtract).then_inc(max_copied, 1)
                    if k in (1, 3) and has(n):
                        transposed_lo(s, k // 2)
                    if k in (2, 4) and has(n):
                        i = k // 2 - 1
                        projected_lo(s, i, bk_sb, acc[i], k_hi_ready, k_lo_ready)
                    if k in (6, 8) and has(n - 1):
                        values_rest(s - 1, n - 1, (k - 6) // 2)
                    if k in (5, 7) and has(n - 3):
                        output_lo(s - 3, (k - 5) // 2)
                    if k in (10, 12) and has(n):
                        i = (k - 10) // 2
                        projected_lo(s, i, bq_sb, acc[i], q_hi_ready, q_lo_ready)
                    for u in scored(n, k):
                        maximum(s - 1, n - 1, u)
                    if k == 12 and has(n + 1):
                        dve.wait_ge(ln_step, 5 * (s + 1) + T)
                        if n >= 0:
                            dve.wait_ge(xn_ready, 2 * (s + 1))
                    if k in (0, 2) and has(n - 3):
                        normalise(s - 3, n - 3, G - 2 + k // 2)
                    if 4 <= k and k % 2 == 0 and has(n - 2):
                        normalise(s - 2, n - 2, k // 2 - 2)
                    if k in (7, 9) and has(n - 1):
                        values_3(s - 1, n - 1, (k - 7) // 2)
                    if k == 11 and has(n + 1):
                        statistics(s + 1, n + 1)
                    if k == 12 and has(n + 1):
                        variance(s + 1)
                    if k == 15 and has(n + 1):
                        layer_norm(s + 1)
                    if (n, k) in ((-1, 14), (-1, 15), (0, 6)):
                        w = "kqv"[((-1, 14), (-1, 15), (0, 6)).index((n, k))]
                        dve.wait_ge(w_hi_ready[w], 1)
                        split_lo(w, raw[w], w_lo_ready[w])
                    if n == 1:
                        output_weights(k)
                    if n >= B:
                        mix_weights_ready(n, k)
                    if k == 14 and has(n - 3):
                        residual(s - 3, 0)

            run(dve, step)
            dve.wait_ge(mix_ready, 5)

        @block.tensor
        def _(pe):
            def scores_t(b, n, u):
                if n <= 1 and u == 0:
                    pe.wait_ge(minus_rows, 2)
                if u == 0:
                    pe.wait_ge(max_stacked, 2 * DMA_INC * (b + 1))
                if n > 0 or u >= 2:
                    pe.wait_ge(probs_ready, H * b + u - 1)
                for t in range(T):
                    last = nc.tensor.matmul(st_bank[u % 2][:, t * S:(t + 1) * S],
                                            k_stack[n % 2][0:SROWS, u, t * P:(t + 1) * P],
                                            q_stack[n % 2][0:SROWS, u, :], start=True, stop=True)
                last.then_inc(st_psum, 1)

            def weighted(b, n, u):
                grp = u // HG
                if n == 0 and u == 0:
                    pe.wait_ge(bias_ready, 2)
                if u == 0:
                    pe.wait_ge(v_ready, 2 * b + 2)
                if u % HG == 0 and (n > 0 or grp >= 2):
                    pe.wait_ge(pv_read, 2 * (G * b + grp - 1))
                pe.wait_ge(probs_lo_ready, H * b + u + 1)
                for j in range(T):
                    at = ((u % HG) * T + j) * VW
                    out = pv_bank[grp % 2][:, at:at + VW]
                    cols = slice(j * P, (j + 1) * P)
                    for t in range(T):
                        v = v_sb[n % 2][:, t, u, :]
                        nc.tensor.matmul(out, probs_hi[u % 2][:, t, cols], v, start=(t == 0), stop=False)
                        last = nc.tensor.matmul(out, probs_lo[u % 2][:, t, cols], v, start=False, stop=(t == T - 1))
                last.then_inc(pv_psum, 1)

            def scores(b, n, u):
                if u == 0:
                    pe.wait_ge(k_stacked[0], STACK * (b + 1))
                    pe.wait_ge(q_stacked[0], STACK * (b + 1))
                    if n > 0:
                        pe.wait_ge(max_copied, 2 * b)
                elif u == H // 2:
                    pe.wait_ge(k_stacked[1], STACK * (b + 1))
                    pe.wait_ge(q_stacked[1], STACK * (b + 1))
                if n > 0 or u >= 2:
                    pe.wait_ge(max_ready, H * b + u - 1)
                for j in range(T):
                    last = nc.tensor.matmul(s_bank[u % 2][:, j * S:(j + 1) * S],
                                            q_stack[n % 2][0:KROWS, u, j * P:(j + 1) * P],
                                            k_stack[n % 2][0:KROWS, u, :], start=True, stop=True)
                last.then_inc(s_psum, 1)

            def maxima(b, n):
                pe.wait_ge(max_ready, H * (b + 1))
                nc.tensor.transpose(s_bank[0][0:H * T, 0:P], row_max[:, :, :].rearrange("p h j -> p (h j)"),
                                    eye_sb[:, :]).then_inc(max_psum, 1)

            def transpose_x(s, n, j):
                if j == 0:
                    if has(n - 4):
                        pe.wait_ge(x1_ready, 2 * (s - 4) + 2)
                    elif n >= 1:
                        pe.wait_ge(q_lo_ready, 2 * s)
                else:
                    pe.wait_ge(k_lo_ready, 2 * s + 1)
                pe.wait_ge(xn_ready, 2 * s + j + 1)
                for c in range(C):
                    last = nc.tensor.transpose(acc[1 - j][:, c * P:(c + 1) * P], x_sb[j][:, c * P:(c + 1) * P],
                                               eye_sb[:, :])
                last.then_inc(xt_psum, 1)

            def transposed_product(w, act_hi, act_lo, pair, bank, half):
                c = 2 * pair + half
                cols = slice(c * P, (c + 1) * P)
                out = bank[:, half * S:(half + 1) * S]
                for i in range(C):
                    nc.tensor.matmul(out, w_hi[w][:, i, cols], act_hi[:, i, :], start=(i == 0), stop=False)
                    nc.tensor.matmul(out, w_hi[w][:, i, cols], act_lo[:, i, :], start=False, stop=False)
                    last = nc.tensor.matmul(out, w_lo[w][:, i, cols], act_hi[:, i, :], start=False, stop=(i == C - 1))
                return last

            def keys(s, n, pair, half):
                if half == 0:
                    if pair == 0:
                        if n == 0:
                            pe.wait_ge(w_lo_ready["k"], 1)
                        pe.wait_ge(ctx_lo_ready, 2 * (s + 1))
                        if has(n - 4):
                            pe.wait_ge(x1_ready, 2 * (s - 4) + 1)
                        elif n >= 1:
                            pe.wait_ge(q_lo_ready, 2 * s - 1)
                    else:
                        pe.wait_ge(xt_lo, 2 * s + 1)
                last = transposed_product("k", ctx_hi[n % 2], ctx_lo[n % 2], pair, acc[pair], half)
                if half == 1:
                    last.then_inc(k_psum, 1)

            def queries(s, n, pair, half):
                if half == 0:
                    if pair == 0:
                        if n == 0:
                            pe.wait_ge(w_lo_ready["q"], 1)
                        pe.wait_ge(xt_lo, 2 * s + 2)
                        if has(n - 3):
                            pe.wait_ge(ot_lo, 2 * (s - 3) + 2)
                        elif has(n - 1):
                            pe.wait_ge(v_rest, 2 * s - 1)
                    elif has(n - 1):
                        pe.wait_ge(v_rest, 2 * s)
                    else:
                        pe.wait_ge(k_lo_ready, 2 * s + 2)
                last = transposed_product("q", xn_hi, xn_lo, pair, acc[pair], half)
                if half == 1:
                    last.then_inc(q_psum, 1)

            def token_product(w, act_hi, act_lo, bank, half, start, stop):
                for i in (2 * half, 2 * half + 1):
                    nc.tensor.matmul(bank[:, :], act_hi(i), w_hi[w][:, i, :], start=(start and i == 0), stop=False)
                    nc.tensor.matmul(bank[:, :], act_hi(i), w_lo[w][:, i, :], start=False, stop=False)
                    last = nc.tensor.matmul(bank[:, :], act_lo(i), w_hi[w][:, i, :], start=False,
                                            stop=(stop and i == C - 1))
                return last

            def values(s, n, j, half):
                if n == 1 and j == 0 and half == 0:
                    pe.wait_ge(w_lo_ready["v"], 1)
                if half == 0:
                    if j == 0:
                        if has(n):
                            pe.wait_ge(xt_lo, 2 * s + 2)
                        else:
                            pe.wait_ge(x1_ready, 2 * (s - 4) + 1)
                    elif has(n - 3):
                        pe.wait_ge(ot_lo, 2 * (s - 3) + 1)
                    else:
                        pe.wait_ge(k_lo_ready, 2 * s + 2)
                par, at = (n - 1) % 2, slice(j * P, (j + 1) * P)
                last = token_product("v", lambda i: ctx_hi[par][:, i, at], lambda i: ctx_lo[par][:, i, at],
                                     acc[j], half, True, True)
                if half == 1:
                    last.then_inc(v_psum, 1)

            def transpose_o(s, n, j):
                if j == 0:
                    if has(n):
                        pe.wait_ge(k_lo_ready, 2 * s + 2)
                    elif has(n - 4):
                        pe.wait_ge(x1_ready, 2 * (s - 4) + 2)
                    pe.wait_ge(o_ready, G * (s - 2))
                elif has(n - 1):
                    pe.wait_ge(v_rest, 2 * s - 1)
                elif has(n - 4):
                    pe.wait_ge(x1_ready, 2 * (s - 4) + 1)
                for c in range(C):
                    last = nc.tensor.transpose(acc[1 - j][:, c * P:(c + 1) * P], o_chunk(n - 3, c)[:, j, :, :].rearrange("p h d -> p (h d)"),
                                               eye_sb[:, :])
                last.then_inc(ot_psum, 1)

            def output(s, n, j, half):
                if n == 3 and j == 0 and half == 0:
                    pe.wait_ge(w_lo_ready["o"], 1)
                if half == 0:
                    pe.wait_ge(ot_lo, 2 * (s - 3) + (2 if j == 0 else 2))
                    if has(n):
                        pe.wait_ge(q_lo_ready, 2 * s + j + 1)
                    elif has(n - 1) and j == 1:
                        pe.wait_ge(v_rest, 2 * s)
                last = token_product("o", lambda i: o_hi[j][:, i, :], lambda i: o_lo[j][:, i, :],
                                     acc[j], half, True, True)
                if half == 1:
                    last.then_inc(o_psum, 1)

            def step(s, n):
                for k in range(H):
                    if n == 2 and k == 0:
                        for half in range(2):
                            keys(s, n, 0, half)
                    if has(n - 2):
                        scores_t(s - 2, n - 2, k)
                    if k < 2 and has(n - 3):
                        weighted(s - 3, n - 3, H - 2 + k)
                    if k >= 2 and has(n - 2):
                        weighted(s - 2, n - 2, k - 2)
                    now = scored(n, k)
                    if k in (1, 3) and has(n):
                        transpose_x(s, n, k // 2)
                    if k in (5, 7) and has(n - 3):
                        transpose_o(s, n, (k - 5) // 2)
                    for u in now[:1]:
                        scores(s - 1, n - 1, u)
                    if k < 4 and has(n) and not (n == 2 and k < 2):
                        keys(s, n, k // 2, k % 2)
                    if 4 <= k < 8 and has(n - 1):
                        values(s, n, (k - 4) // 2, k % 2)
                    if 8 <= k < 12 and has(n):
                        queries(s, n, (k - 8) // 2, k % 2)
                    if k >= 12 and has(n - 3):
                        output(s, n, (k - 12) // 2, k % 2)
                    for u in now[1:]:
                        scores(s - 1, n - 1, u)
                    if k == 12 and has(n - 1):
                        maxima(s - 1, n - 1)
                    if n == 1 and k in (2, 6):
                        output_bias(k)

            def output_bias(k):
                if k == 2:
                    pe.wait_ge(gated, 1)
                    for c in range(C):
                        last = nc.tensor.matmul(pv_bank[0][0:1, :], bv_sb[:, c:c + 1], raw["o"][:, c, :],
                                                start=(c == 0), stop=(c == C - 1))
                    last.then_inc(bias_psum, 1)
                else:
                    pe.wait_ge(bias_ready, 1)
                    nc.tensor.matmul(pv_bank[1][:, :], ones_row, out_bias[0:1, :], start=True, stop=True)\
                        .then_inc(bias_psum, 1)

            pe.wait_ge(consts, 4)
            pe.wait_ge(biases_in, 3 * DMA_INC)
            run(pe, step)


def channel_mix_pass(nc, psum, w_hi, w_lo, eye_sb, minus_half, mu, one_minus_mu, x1, out):
    B, S, D = x1.shape
    C = D // P
    TP = 2 * S
    T = TP // P
    STEPS = B // 2
    assert TP == BANK and C == 4 and T == 4

    with ExitStack() as scope:
        def sb(name, shape, dt):
            return scope.enter_context(nc.sbuf_tensor(name, shape, dt))

        def sem(name):
            return scope.enter_context(nc.semaphore(name))

        x_sb = [[sb(f"y{i}_sb{j}", [P, D], F32) for j in range(T)] for i in range(2)]
        stats = sb("stats_f", [P, T, 6], F32)
        mean_var = sb("mean_var_f", [P, T, 2], F32)
        var_eps = sb("var_eps_f", [P, T], F32)
        rstd = sb("rstd_f", [P, T], F32)
        xn = sb("xn_f", [P, T, D], F32)
        xt = sb("xt_f", [P, C, 2, S + 1], F32)
        mixed = {n: sb(f"mixed_{n}", [P, C, TP], F32) for n in "rk"}
        m_hi = {n: sb(f"m{n}_hi", [P, C, TP], F32R) for n in "rk"}
        m_lo = {n: sb(f"m{n}_lo", [P, C, TP], F32R) for n in "rk"}
        kact = sb("kact", [P, C, TP], F32)
        kact_hi = sb("kact_hi", [P, C, TP], F32R)
        kact_lo = sb("kact_lo", [P, C, TP], F32R)
        tanh_r = sb("tanh_r", [P, T, D], F32)

        kv_bank = psum[0:4]
        r_bank = psum[4:6]
        t_bank = psum[6:8]

        zeroed = sem("zeroed")
        x_in = [[sem(f"y{i}_in{j}") for j in range(T)] for i in range(2)]
        ln_step = sem("ln_step_f")
        rstd_ready = sem("rstd_ready_f")
        xn_ready = sem("xn_ready_f")
        xt_psum = sem("xt_psum_f")
        xt_ready = sem("xt_ready_f")
        k_mixed = sem("k_mixed")
        k_hi = sem("k_hi_f")
        k_lo = sem("k_lo_f")
        r_mixed = sem("r_mixed")
        r_hi = sem("r_hi_f")
        r_lo = sem("r_lo_f")
        k_psum = sem("k_psum_f")
        relu_ready = sem("relu_ready")
        square_ready = sem("square_ready")
        act_hi = sem("act_hi")
        act_lo = sem("act_lo")
        r_psum = sem("r_psum")
        tanh_ready = sem("tanh_ready")
        v_psum = sem("v_psum_f")
        product_ready = sem("product_ready")
        out_ready = sem("out_ready")
        out_sent = [sem(f"out_sent{j}") for j in range(T)]

        FIRST_STEADY = 2
        LAST_STEADY = STEPS - 2
        assert (LAST_STEADY - FIRST_STEADY) % 2 == 0

        def run(eng, step):
            for s in range(-1, FIRST_STEADY):
                step(s, s)
            with eng.Fori(0, (LAST_STEADY - FIRST_STEADY) // 2) as i:
                for j in range(2):
                    step(2 * i + (FIRST_STEADY + j), FIRST_STEADY + j)
            for s in range(LAST_STEADY, STEPS):
                step(s, s)

        def has(n):
            return 0 <= n < STEPS

        def rows(dram, s, j):
            return dram[2 * s + j // 2, (j % 2) * P:(j % 2 + 1) * P, :]

        block = scope.enter_context(nc.Block())

        @block.sync
        def _(sp):
            for j in range(T):
                sp.dma_start(x_sb[0][j][:, :], rows(x1, 0, j)).then_inc(x_in[0][j], DMA_INC)

            def step(s, n):
                for j in range(T):
                    if has(n):
                        sp.wait_ge(out_ready, T * s + j + 1)
                        sp.dma_start(rows(out, s, j), tanh_r[:, j, :]).then_inc(out_sent[j], DMA_INC)
                    if has(n + 2):
                        sp.dma_start(x_sb[n % 2][j][:, :], rows(x1, s + 2, j)).then_inc(x_in[n % 2][j], DMA_INC)

            run(sp, step)
            for j in range(T):
                sp.wait_ge(out_sent[j], DMA_INC * STEPS)

        @block.gpsimd
        def _(pool):
            def step(s, n):
                for c in range(C):
                    if has(n):
                        pool.wait_ge(relu_ready, C * s + c + 1)
                        nc.gpsimd.tensor_tensor(kact[:, c, :], kact[:, c, :], kact[:, c, :], ALU.mult)\
                            .then_inc(square_ready, 1)
                    if c == 0 and has(n + 1):
                        pool.wait_ge(ln_step, 9 * (s + 2))
                        nc.gpsimd.tensor_tensor(rstd[:, :], var_eps[:, :], minus_half[:, 0:T], ALU.pow)\
                            .then_inc(rstd_ready, 1)
                if has(n):
                    for j in range(T):
                        pool.wait_ge(product_ready, T * s + j + 1)
                        nc.gpsimd.tensor_tensor(tanh_r[:, j, :], tanh_r[:, j, :], x_sb[n % 2][j][:, :], ALU.add)\
                            .then_inc(out_ready, 1)

            run(pool, step)

        @block.scalar
        def _(act):
            def relu(s, n, c):
                act.wait_ge(k_psum, C * s + c + 1)
                if n > 0:
                    act.wait_ge(act_lo, C * s + c - C + 1)
                nc.scalar.activation(kact[:, c, :], kv_bank[c][:, :], ACT.Relu).then_inc(relu_ready, 1)

            def square_hi(s, n, c):
                act.wait_ge(square_ready, C * s + c + 1)
                if n > 0:
                    act.wait_ge(v_psum, T * s)
                nc.scalar.activation(kact_hi[:, c, :], kact[:, c, :], ACT.Copy).then_inc(act_hi, 1)

            def tanh(s, n, j):
                act.wait_ge(r_psum, T * s + j + 1)
                if n > 0:
                    act.wait_ge(out_sent[j], DMA_INC * s)
                nc.scalar.activation(tanh_r[:, j, :], r_bank[j % 2][:, :], ACT.Tanh, scale=0.5)\
                    .then_inc(tanh_ready, 1)

            def transposed(s, n, c):
                bank = t_bank[c % 2][:, :]
                act.wait_ge(xt_psum, C * s + c + 1)
                if n > 0:
                    act.wait_ge(r_lo, C * s - C + c + 1)
                nc.scalar.activation(xt[:, c, :, 1:S + 1], bank.rearrange("p (b t) -> p b t", b=2), ACT.Copy)
                nc.scalar.activation(mixed["k"][:, c, :], bank, ACT.Copy, scale=mu["k"][:, c:c + 1])
                nc.scalar.activation(mixed["r"][:, c, :], bank, ACT.Copy, scale=mu["r"][:, c:c + 1])\
                    .then_inc(xt_ready, 1)

            def mixed_hi(s, n, c):
                act.wait_ge(r_mixed, C * s + c + 1)
                nc.scalar.activation(m_hi["r"][:, c, :], mixed["r"][:, c, :], ACT.Copy).then_inc(r_hi, 1)

            def step(s, n):
                if has(n):
                    for c in range(C):
                        relu(s, n, c)
                        if c >= 1:
                            square_hi(s, n, c - 1)
                for c in range(C):
                    if has(n):
                        tanh(s, n, c)
                        if c == 0:
                            square_hi(s, n, C - 1)
                    if has(n + 1):
                        transposed(s + 1, n + 1, c)
                if has(n + 1):
                    for c in range(C):
                        mixed_hi(s + 1, n + 1, c)

            run(act, step)

        @block.vector
        def _(dve):
            nc.vector.memset(xt[:, :, :, 0:1], 0.0).then_inc(zeroed, 1)

            def statistics(s, n):
                x = x_sb[n % 2]
                if n > 0:
                    dve.wait_ge(ln_step, 9 * s)
                for j in range(T):
                    dve.wait_ge(x_in[n % 2][j], DMA_INC // 2 * (s + (2 - n % 2)))
                    nc.vector.bn_stats(stats[:, j, :], x[j][:, :]).then_inc(ln_step, 1)

            def variance(s):
                for j in range(T):
                    nc.vector.bn_aggr(mean_var[:, j, :], stats[:, j, :]).then_inc(ln_step, 1)
                dve.wait_ge(ln_step, 9 * s + 2 * T)
                nc.vector.tensor_scalar(var_eps[:, :], mean_var[:, :, 1], EPS, None, ALU.add).then_inc(ln_step, 1)

            def normalise(s, n):
                dve.wait_ge(rstd_ready, s + 1)
                if n > 0:
                    dve.wait_ge(xt_psum, C * s)
                for j in range(T):
                    nc.vector.tensor_scalar(xn[:, j, :], x_sb[n % 2][j][:, :], mean_var[:, j, 0:1],
                                            rstd[:, j:j + 1], ALU.subtract, ALU.mult).then_inc(xn_ready, 1)

            def square_lo(s, c):
                dve.wait_ge(act_hi, C * s + c + 1)
                nc.vector.tensor_tensor(kact_lo[:, c, :], kact[:, c, :], kact_hi[:, c, :].bitcast(F32),
                                        ALU.subtract).then_inc(act_lo, 1)

            def mix(s, name, c, done):
                m = mixed[name][:, c, :].rearrange("p (b t) -> p b t", b=2)
                nc.vector.scalar_tensor_tensor(out=m, in0=xt[:, c, :, 0:S], scalar=one_minus_mu[name][:, c:c + 1],
                                               in1=m, op0=ALU.mult, op1=ALU.add).then_inc(done, 1)

            def mix_k(s, n, c):
                dve.wait_ge(xt_ready, C * s + c + 1)
                mix(s, "k", c, k_mixed)
                if n > 0 and c == 0:
                    dve.wait_ge(k_psum, C * s)
                dve.wait_ge(k_mixed, C * s + c + 1)
                nc.vector.tensor_copy(m_hi["k"][:, c, :], mixed["k"][:, c, :]).then_inc(k_hi, 1)
                dve.wait_ge(k_hi, C * s + c + 1)
                nc.vector.tensor_tensor(m_lo["k"][:, c, :], mixed["k"][:, c, :], m_hi["k"][:, c, :].bitcast(F32),
                                        ALU.subtract).then_inc(k_lo, 1)

            def mix_r(s, c):
                mix(s, "r", c, r_mixed)

            def mix_r_lo(s, n, c):
                dve.wait_ge(r_hi, C * s + c + 1)
                nc.vector.tensor_tensor(m_lo["r"][:, c, :], mixed["r"][:, c, :], m_hi["r"][:, c, :].bitcast(F32),
                                        ALU.subtract).then_inc(r_lo, 1)

            def product(s, j):
                dve.wait_ge(tanh_ready, T * s + j + 1)
                dve.wait_ge(v_psum, T * s + j + 1)
                nc.vector.scalar_tensor_tensor(out=tanh_r[:, j, :], in0=tanh_r[:, j, :], scalar=1.0,
                                               in1=kv_bank[j][:, :], op0=ALU.add, op1=ALU.mult)\
                    .then_inc(product_ready, 1)

            def step(s, n):
                if has(n + 1):
                    statistics(s + 1, n + 1)
                    dve.wait_ge(ln_step, 9 * (s + 1) + T)
                    if n >= 0:
                        dve.wait_ge(xn_ready, T * (s + 1))
                if has(n):
                    square_lo(s, 0)
                if has(n + 1):
                    variance(s + 1)
                if has(n):
                    square_lo(s, 1)
                if has(n + 1):
                    normalise(s + 1, n + 1)
                if has(n):
                    for c in range(2, C):
                        square_lo(s, c)
                if has(n + 1):
                    for c in range(C):
                        mix_k(s + 1, n + 1, c)
                        if n >= 0:
                            mix_r(s + 1, c)
                    if n < 0:
                        for c in range(C):
                            mix_r(s + 1, c)
                for c in range(C):
                    if has(n + 1):
                        mix_r_lo(s + 1, n + 1, c)
                    if has(n):
                        product(s, c)

            run(dve, step)

        @block.tensor
        def _(pe):
            def keys(s, n, c):
                if n > 0:
                    pe.wait_ge(product_ready, T * s - T + c + 1)
                cols = slice(c * P, (c + 1) * P)
                for i in range(C):
                    if c == 0:
                        pe.wait_ge(k_lo, C * s + i + 1)
                    nc.tensor.matmul(kv_bank[c][:, :], w_hi["k"][:, i, cols], m_hi["k"][:, i, :],
                                     start=(i == 0), stop=False)
                    nc.tensor.matmul(kv_bank[c][:, :], w_hi["k"][:, i, cols], m_lo["k"][:, i, :],
                                     start=False, stop=False)
                    last = nc.tensor.matmul(kv_bank[c][:, :], w_lo["k"][:, i, cols], m_hi["k"][:, i, :],
                                            start=False, stop=(i == C - 1))
                last.then_inc(k_psum, 1)

            def token_product(w, hi, lo, bank, j):
                at = slice(j * P, (j + 1) * P)
                for i in range(C):
                    nc.tensor.matmul(bank[:, :], hi[:, i, at], w_hi[w][:, i, :], start=(i == 0), stop=False)
                    nc.tensor.matmul(bank[:, :], hi[:, i, at], w_lo[w][:, i, :], start=False, stop=False)
                    last = nc.tensor.matmul(bank[:, :], lo[:, i, at], w_hi[w][:, i, :], start=False,
                                            stop=(i == C - 1))
                return last

            def receptance(s, n, j):
                if j == 0:
                    pe.wait_ge(r_lo, C * (s + 1))
                if n > 0 or j >= 2:
                    pe.wait_ge(tanh_ready, T * s + j - 1)
                token_product("r", m_hi["r"], m_lo["r"], r_bank[j % 2], j).then_inc(r_psum, 1)

            def values(s, n, j):
                if j == 0:
                    pe.wait_ge(act_lo, C * (s + 1))
                pe.wait_ge(relu_ready, C * s + j + 1)
                token_product("v", kact_hi, kact_lo, kv_bank[j], j).then_inc(v_psum, 1)

            def transposes(s, n, c):
                if c == 0:
                    pe.wait_ge(xn_ready, T * (s + 1))
                if n > 0 or c >= 2:
                    pe.wait_ge(xt_ready, C * s + c - 1)
                for j in range(T):
                    last = nc.tensor.transpose(t_bank[c % 2][:, j * P:(j + 1) * P], xn[:, j, c * P:(c + 1) * P],
                                               eye_sb[:, :])
                last.then_inc(xt_psum, 1)

            def step(s, n):
                if has(n):
                    for c in range(C):
                        keys(s, n, c)
                for j in range(C):
                    if has(n):
                        receptance(s, n, j)
                    if has(n + 1):
                        transposes(s + 1, n + 1, j)
                if has(n):
                    for j in range(T):
                        values(s, n, j)

            run(pe, step)


def build(nc, x, ctx_t, g_a, wq_t, bq, wk_t, bk, wv_t, bv, wo_t, bo, g_f, fr_t, fk_t, fv_t, mu_r, mu_k, eye,
          parts_dram, x1, out):
    D = x.shape[2]
    C = D // P
    with ExitStack() as scope:
        def sb(name, shape, dt):
            return scope.enter_context(nc.sbuf_tensor(name, shape, dt))

        psum = [scope.enter_context(nc.psum_tensor(f"bank{i}", [P, BANK], F32)) for i in range(8)]
        w_hi = {n: sb(f"w{n}_hi", [P, C, D], F32R) for n in "qkvo"}
        w_lo = {n: sb(f"w{n}_lo", [P, C, D], F32R) for n in "qkvo"}
        eye_sb = sb("eye_sb", [P, P], F32)
        minus_half = sb("minus_half", [P, 4], F32)
        gate_f = sb("gate_f", [P, 1], F32)
        mu = {n: sb(f"mu_{n}_sb", [P, C], F32) for n in "rk"}
        one_minus_mu = {n: sb(f"one_minus_mu_{n}", [P, C], F32) for n in "rk"}
        mix_weights = dict(small=((gate_f, g_f), (mu["r"], mu_r), (mu["k"], mu_k)), gate=gate_f,
                           mu=[(mu[n], one_minus_mu[n]) for n in "rk"], r=fr_t, k=fk_t, v=fv_t)
        attention_pass(nc, psum, w_hi, w_lo, eye_sb, minus_half, mix_weights, x, ctx_t, g_a, wq_t, bq, wk_t, bk, wv_t,
                       bv, wo_t, bo, eye, parts_dram, x1)
        mix_hi, mix_lo = ({"r": w["q"], "k": w["k"], "v": w["v"]} for w in (w_hi, w_lo))
        channel_mix_pass(nc, psum, mix_hi, mix_lo, eye_sb, minus_half, mu, one_minus_mu, x1, out)


def kernel(**inputs):
    import numpy as _np
    import concourse.bacc as _bacc
    from concourse import mybir as _mybir
    from concourse.bass_utils import run_bass_kernel_spmd as _run

    a = {n: _np.asarray(v) for n, v in inputs.items()}
    B, S, D = a["x"].shape

    def t(w):
        return _np.ascontiguousarray(w.T)

    def column(v):
        return _np.ascontiguousarray(v.reshape(D // P, P).T)

    def everywhere(v):
        return _np.ascontiguousarray(_np.broadcast_to(v.reshape(1, 1), (P, 1)))

    data = dict(
        x=a["x"], ctx_t=_np.ascontiguousarray(a["ctx_1024"].transpose(0, 2, 1)), g_a=everywhere(a["g_xattn"]),
        wq_t=t(a["L0_xattn_Wq"]), bq=column(a["L0_xattn_bq"]), wk_t=t(a["L0_xattn_Wk"]), bk=column(a["L0_xattn_bk"]),
        wv_t=t(a["L0_xattn_Wv"]), bv=column(a["L0_xattn_bv"]), wo_t=t(a["L0_xattn_Wo"]),
        bo=_np.ascontiguousarray(a["L0_xattn_bo"].reshape(1, D)), g_f=everywhere(a["g_ffn"]),
        fr_t=t(a["L0_ffn_W_r"]), fk_t=t(a["L0_ffn_W_k"]), fv_t=t(a["L0_ffn_W_v"]),
        mu_r=column(a["L0_ffn_mu_r"]), mu_k=column(a["L0_ffn_mu_k"]), eye=_np.eye(P, dtype=_np.float32),
    )
    nc = _bacc.Bacc("TRN2", target_bir_lowering=False, num_devices=1)
    arrays, args = {}, {}
    for name, v in data.items():
        v = _np.ascontiguousarray(v)
        arrays[f"in_{name}"] = v
        args[name] = nc.dram_tensor(f"in_{name}", v.shape, _mybir.dt.from_np(v.dtype), kind="ExternalInput").ap()
    args["x1"] = nc.dram_tensor("x1_dram", (B, S, D), F32, kind="Internal").ap()
    args["parts_dram"] = nc.dram_tensor("parts_dram", (2, 2, D, 2, S), F32, kind="Internal").ap()
    args["out"] = nc.dram_tensor("out_0", (B, S, D), F32, kind="ExternalOutput").ap()
    build(nc, **args)
    r = _run(nc, [arrays], core_ids=[0])
    return r.results[0]["out_0"]
```
